# Optimizing a Trainium2 kernel written in Bass

```python
import numpy as np
import jax
import jax.numpy as jnp

def _softmax(x, axis=-1):
    return jax.nn.softmax(x, axis=axis)

def _gelu(x):
    return jax.nn.gelu(x, approximate=True)

def _silu(x):
    return jax.nn.silu(x)

def _sigmoid(x):
    return jax.nn.sigmoid(x)

def _layernorm(x, axis=-1, eps=1e-05):
    m = jnp.mean(x, axis=axis, keepdims=True)
    v = jnp.var(x, axis=axis, keepdims=True)
    return (x - m) / jnp.sqrt(v + eps)

def _scatter_add(tgt, idx, src, axis=0):
    return tgt.at[idx].add(src)

def _segment_sum(src, seg, n):
    return jax.ops.segment_sum(src, seg, n)
kernel_name = 'mk_prb_d1_jaxref_r4_40b166'

def setup_inputs(seed: int=0):
    np.random.seed(seed)
    _w = jnp.asarray

    def _L0_attn_setup():
        import jax, jax.numpy as jnp
        import numpy as np
        import math
        FACTOR = 1
        key = jax.random.key(seed)
        x = jax.random.normal(key, (8, 128, 1024), dtype=jnp.float32)
        return {'x': x}
    _L0_attn_in = _L0_attn_setup()

    def _L0_ffn_setup():
        import jax, jax.numpy as jnp
        import numpy as np
        _TRIPLES = [(1, 2, 3), (1, 4, 5), (1, 7, 6), (2, 4, 6), (2, 5, 7), (3, 4, 7), (3, 6, 5)]

        def _oct_struct():
            S = np.zeros((8, 8, 8), np.float32)
            S[0, 0, 0] = 1.0
            for i in range(1, 8):
                S[0, i, i] = 1.0
                S[i, 0, i] = 1.0
                S[i, i, 0] = -1.0
            for a, b, c in _TRIPLES:
                for x, y, z in ((a, b, c), (b, c, a), (c, a, b)):
                    S[x, y, z] = 1.0
                    S[y, x, z] = -1.0
            return jnp.asarray(S)
        S_OCT = _oct_struct()
        N_EMBD = 1024
        HIDDEN = 2732

        def ternary_dequant(W):
            scale = jnp.mean(jnp.abs(W))
            Wq = scale * jnp.clip(jnp.round(W / scale), -1.0, 1.0)
            return W + jax.lax.stop_gradient(Wq - W)

        def oct_ternary_linear(xp, W):
            Wq = ternary_dequant(W)
            M = jnp.einsum('jik,jod->koid', S_OCT, Wq)
            return jnp.einsum('...id,koid->...ko', xp, M)
        key = jax.random.key(seed)
        k1, k2, k3, k4 = jax.random.split(key, 4)
        B, T = (2, 512)
        d8, h8 = (N_EMBD // 8, HIDDEN // 8)
        std_in = 1.0 / np.sqrt(N_EMBD)
        std_h = 1.0 / np.sqrt(HIDDEN)
        return {'x': jax.random.normal(k1, (B, T, N_EMBD), jnp.float32), 'w_gate': jax.random.normal(k2, (8, h8, d8), jnp.float32) * std_in, 'w_up': jax.random.normal(k3, (8, h8, d8), jnp.float32) * std_in, 'w_down': jax.random.normal(k4, (8, d8, h8), jnp.float32) * std_h}
    _L0_ffn_in = _L0_ffn_setup()
    _d = {'L0_attn_x': _L0_attn_in['x'], 'L0_ffn_w_gate': _L0_ffn_in['w_gate'], 'L0_ffn_w_up': _L0_ffn_in['w_up'], 'L0_ffn_w_down': _L0_ffn_in['w_down']}
    _x0 = _d['L0_attn_x']
    _d['L0_attn_x'] = jax.random.normal(jax.random.fold_in(jax.random.key(seed), 1), (1, 2048, 1024), dtype=_x0.dtype)
    del _x0
    return _d

def reference(L0_attn_x, L0_ffn_w_gate, L0_ffn_w_up, L0_ffn_w_down):

    def _L0_attn_ref(x):
        import jax, jax.numpy as jnp
        import numpy as np
        import math
        FACTOR = 1
        B, C, L = x.shape
        xh = x[:, None]
        f = jnp.fft.rfft(xh, axis=-1)
        corr = jnp.fft.irfft(f * jnp.conj(f), n=L, axis=-1)
        top_k = int(FACTOR * math.log(L))
        weights, delay = jax.lax.top_k(corr, top_k)
        tmp_corr = jax.nn.softmax(weights, axis=-1)
        init_index = jnp.arange(L)
        idx = (init_index[None, None, None, None, :] + delay[..., None]) % L
        pattern = jnp.take_along_axis(xh[:, :, :, None, :], idx, axis=-1)
        delays_agg = jnp.sum(pattern * tmp_corr[..., None], axis=-2)
        return delays_agg[:, 0]

    def _L0_ffn_ref(x, w_gate, w_up, w_down):
        import jax, jax.numpy as jnp
        import numpy as np
        _TRIPLES = [(1, 2, 3), (1, 4, 5), (1, 7, 6), (2, 4, 6), (2, 5, 7), (3, 4, 7), (3, 6, 5)]

        def _oct_struct():
            S = np.zeros((8, 8, 8), np.float32)
            S[0, 0, 0] = 1.0
            for i in range(1, 8):
                S[0, i, i] = 1.0
                S[i, 0, i] = 1.0
                S[i, i, 0] = -1.0
            for a, b, c in _TRIPLES:
                for x, y, z in ((a, b, c), (b, c, a), (c, a, b)):
                    S[x, y, z] = 1.0
                    S[y, x, z] = -1.0
            return jnp.asarray(S)
        S_OCT = _oct_struct()
        N_EMBD = 1024
        HIDDEN = 2732

        def ternary_dequant(W):
            scale = jnp.mean(jnp.abs(W))
            Wq = scale * jnp.clip(jnp.round(W / scale), -1.0, 1.0)
            return W + jax.lax.stop_gradient(Wq - W)

        def oct_ternary_linear(xp, W):
            Wq = ternary_dequant(W)
            M = jnp.einsum('jik,jod->koid', S_OCT, Wq)
            return jnp.einsum('...id,koid->...ko', xp, M)
        B, T, D = x.shape
        xp = x.reshape(B, T, 8, D // 8)
        gate = oct_ternary_linear(xp, w_gate).reshape(B, T, -1)
        up = oct_ternary_linear(xp, w_up).reshape(B, T, -1)
        h = jax.nn.silu(gate) * up
        hp = h.reshape(B, T, 8, h.shape[-1] // 8)
        out = oct_ternary_linear(hp, w_down).reshape(B, T, D)
        return out
    x = L0_attn_x
    xn = _layernorm(x, axis=-1)
    x = x + _L0_attn_ref(xn) + _L0_ffn_ref(xn, L0_ffn_w_gate, L0_ffn_w_up, L0_ffn_w_down)
    return x

_drawn_inputs = setup_inputs


def setup_inputs(seed=0):
    import zlib

    import numpy as np

    out = dict(_drawn_inputs(seed))
    spreads = {}
    factors = {}
    for name, (base, spread) in spreads.items():
        noise = np.random.default_rng([zlib.crc32(name.encode()), seed]).standard_normal(out[name].shape)
        drawn = base * np.exp(spread * noise) if base else spread * noise
        out[name] = jnp.asarray(drawn.astype(out[name].dtype))
    for name, factor in factors.items():
        out[name] = (out[name] * factor).astype(out[name].dtype)
    return out
```

```python
def octonion_ffn_attention_kernel(nc, x, w_gate, w_up, w_down, dft, lag, out):
    import concourse.bass as bass
    from concourse import mybir
    from contextlib import ExitStack

    F32, F16, I32 = mybir.dt.float32, mybir.dt.float16, mybir.dt.int32
    ALU, ACT, AX = mybir.AluOpType, mybir.ActivationFunctionType, mybir.AxisListType

    P = 128
    ROWS, D = x.shape
    NJ, HB, DB = w_gate.shape
    QN = NJ // 2
    NC = 3
    CH = -(-HB // NC)
    HW = NC * CH
    T = 512
    NT = T // P
    G = ROWS // T
    NU = NC * QN
    N_W = NJ * HB * DB
    EPS = 1e-5
    XS = 1024.0
    HS = 2.0 ** -6
    MARGIN = 150.0
    LAG_SCALE = 16.0
    TOP = 6
    STEPS = 35
    DELTA = (1, -1, -1, 1)

    sign = [[0] * NJ for _ in range(NJ)]
    for i in range(NJ):
        sign[0][i] = sign[i][0] = 1
        if i:
            sign[i][i] = -1
    for a, b, c in [(1, 2, 3), (1, 4, 5), (1, 7, 6), (2, 4, 6), (2, 5, 7), (3, 4, 7), (3, 6, 5)]:
        for u, v in ((a, b), (b, c), (c, a)):
            sign[u][v], sign[v][u] = 1, -1
    products = []
    for k in range(QN):
        of_k = []
        for q in range(QN):
            p = k ^ q
            a, b, c, d = sign[p][q], sign[p + 4][q + 4], sign[p + 4][q], sign[p][q + 4]
            if a * d == DELTA[k]:
                of_k.append([(0, 2, (p, a, 0)), (1, 1, (p, -a, b)), (2, 0, (p, -d, c))])
            else:
                of_k.append([(0, 2, (p, 0, b)), (1, 0, (p, a, -b)), (2, 1, (p, d, -c))])
        products.append(of_k)
    slots = sorted({w for of_k in products for of_q in of_k for _, _, w in of_q})
    slot_of = {w: n for n, w in enumerate(slots)}
    NS = len(slots)

    ctx = ExitStack()
    with ctx:
        def sb(name, shape, dt):
            return ctx.enter_context(nc.sbuf_tensor(name, shape, dt))

        def sem(name):
            return ctx.enter_context(nc.semaphore(name))

        wg = sb("wg", [P, NS, HW], F16)
        wu = sb("wu", [P, NS, HW], F16)
        wd = sb("wd", [CH, NS, NC, DB], F16)
        xop = sb("xop", [P, QN, 3, 2, T], F16)
        hop = sb("hop", [P, NC, QN, 3, 2, T], F16)
        xr = sb("xr", [P, NT, D], F32)
        zx = sb("zx", [P, 2, 2, NT, DB], F32)
        zt = sb("zt", [P, 2, NT, DB], F32)
        kb = sb("kb", [P, T], F32)
        gb = sb("gb", [CH, 2, T], F32)
        hh = sb("hh", [CH, 3, T], F32)
        yt = sb("yt", [P, 2, T], F32)
        pw = yt[:, :, :].bitcast(F16).rearrange("p b (m t) -> p (b m) t", t=T)
        xs = sb("xs", [P, T], F32)
        ss = sb("ss", [P, T], F32)
        junk = sb("junk", [P, D], F16)
        dft_sb = sb("dft_sb", [P, QN, T], F16)
        lag_sb = sb("lag_sb", [P, QN, 256], F16)
        ident = sb("ident", [P, P], F32)
        ident16 = sb("ident16", [P, P], F16)
        ones = sb("ones", [P, P], F32)
        asum = sb("asum", [P, 3, 2], F32)
        tot = sb("tot", [P, 3], F32)
        thr = sb("thr", [P, 3], F32)
        nthr = sb("nthr", [P, 3], F32)
        gsc = sb("gsc", [P, 1], F32)
        hsc = sb("hsc", [P, 1], F32)
        osc = sb("osc", [P, 1], F32)
        sm = sb("sm", [P, NT], F32)
        nm = sb("nm", [P, NT], F32)
        vr = sb("vr", [P, NT], F32)
        r0 = sb("r0", [P, NT], F32)
        rr = sb("rr", [P, NT], F32)
        rs = sb("rs", [P, NT], F32)
        nmd = sb("nmd", [P, NT], F32)
        rsd = sb("rsd", [P, NT], F32)
        mh = sb("mh", [P, NT], F32)
        dmin = sb("dmin", [P, NT], F32)
        rmin = sb("rmin", [P, NT], F32)
        dh = sb("dh", [P, NT], F32)
        rh = sb("rh", [P, NT], F32)
        fl = sb("fl", [P, 2, NT], F32)
        fs = sb("fs", [P, 1], F32)
        flag = sb("flag", [P, 1], I32)
        pz = sb("pz", [P, 1], F32)
        junk2 = sb("junk2", [P, T], F16)

        prep = hop[:, :, :, :, :, :].rearrange("p c k o h t -> p (c k o h t)")
        stage, tern, wt = [], [], []
        for m in range(3):
            stage.append(prep[:, 6144 * m:6144 * (m + 1)].bitcast(F32))
            tern.append(prep[:, 18432 + 3072 * m:18432 + 3072 * (m + 1)])
            wt.append(prep[:, 27648 + 3072 * m:27648 + 3072 * (m + 1)])

        slow = prep.bitcast(F32)
        slow_x = slow[:, 0:D]
        slow_out = slow[:, D:2 * D]
        slow_corr = slow[:, 2 * D:3 * D]
        slow_w = slow[:, 3 * D:4 * D]
        slow_xx = slow[:, 4 * D:6 * D]
        slow_acc = slow[:, 6 * D:7 * D]
        slow_junk = slow[:, 7 * D:8 * D]
        slow_mask = slow[:, 8 * D:9 * D]
        slow_top = slow[:, 9 * D:9 * D + 8]
        slow_neg = slow[:, 9 * D + 8:9 * D + 9]
        slow_st = slow[:, 9 * D + 16:9 * D + 32]

        acc = ctx.enter_context(nc.psum_tensor("acc", [P, 2, 3, T], F32))
        side = ctx.enter_context(nc.psum_tensor("side", [P, 2, T], F32))

        x_in = [sem(f"x_in{t}") for t in range(NT)]; w_in = [sem(f"w_in{m}") for m in range(3)]; tab_in = sem("tab_in"); zx_in = [sem(f"zx_in{n}") for n in range(2)]
        const_done = sem("const_done"); abs_done = sem("abs_done"); total_done = sem("total_done")
        tern_done = sem("tern_done"); wt_mm = sem("wt_mm"); wt_copied = sem("wt_copied"); kslot_done = sem("kslot_done")
        down_ready = sem("down_ready")
        sum_done = sem("sum_done"); mean_done = sem("mean_done"); var_done = sem("var_done"); v_done = sem("v_done")
        guess_done = sem("guess_done"); ln_done = sem("ln_done")
        tr_mm = sem("tr_mm"); tr_hi = sem("tr_hi"); tr_sum = sem("tr_sum"); tr_sumhi = sem("tr_sumhi"); x_ready = sem("x_ready")
        gate_mm = sem("gate_mm"); up_mm = sem("up_mm"); down_mm = sem("down_mm"); k_copied = sem("k_copied")
        acc0_read = sem("acc0_read"); acc1_read = sem("acc1_read"); silu_done = sem("silu_done"); h_done = sem("h_done")
        h_sum = sem("h_sum"); h_hi = sem("h_hi"); h_ready = sem("h_ready")
        dft_mm = sem("dft_mm"); power_done = sem("power_done"); lag_mm = sem("lag_mm"); bound_done = sem("bound_done")
        back_mm = sem("back_mm"); z_done = sem("z_done"); out_done = sem("out_done"); out_st = sem("out_st")
        chain = sem("chain"); pchain = sem("pchain"); flag_sum = sem("flag_sum"); flag_mm = sem("flag_mm"); flag_done = sem("flag_done")
        s_sem = {n: sem("slow_" + n) for n in ("x_in", "ex_in", "dve", "act", "st", "ob")}
        pool_tick = sem("pool_tick"); dve_tick = sem("dve_tick")
        kept = sem("kept")
        least_done = sem("least_done")
        s_half = sem("s_half"); z_part = sem("z_part")
        s_lag = sem("slow_lag"); s_add = sem("slow_add")
        acc_read = (acc0_read, acc1_read)
        PER = NU + 2

        x_rows = x.rearrange("(n p) d -> n p d", p=P)
        out_rows = out.rearrange("(n p) d -> n p d", p=P)
        block = ctx.enter_context(nc.Block())

        def pair_slice(ap, g, k, b):
            return ap[bass.ds(T * g, T), (QN * b + k) * DB:(QN * b + k + 1) * DB].rearrange("(t p) c -> p t c", p=P)

        @block.sync
        def _(sp):
            for t in range(NT):
                sp.dma_start(xr[:, t, :], x_rows[t, :, :]).then_inc(x_in[t], 16)
            for k in range(2):
                for b in range(2):
                    sp.dma_start(zx[:, k, b, :, :], pair_slice(x, 0, k, b)).then_inc(zx_in[k], 16)
            sp.dma_start(dft_sb[:, :, :], dft).then_inc(tab_in, 16)
            sp.dma_start(lag_sb[:, :, :], lag).then_inc(tab_in, 16)

            def group(g, more):
                if more:
                    sp.wait_ge(tr_mm, QN * g + QN)
                    for t in range(NT):
                        sp.dma_start(xr[:, t, :], x[bass.ds(T * g + T + P * t, P), :]).then_inc(x_in[t], 16)
                for k in range(QN):
                    sp.wait_ge(out_done, QN * g + k + 2)
                    for b in range(2):
                        sp.dma_start(pair_slice(out, g, k, b), zx[:, k % 2, b, :, :]).then_inc(out_st, 16)
                    if k + 2 < QN or more:
                        sp.wait_ge(out_st, 32 * (QN * g + k + 1))
                        for b in range(2):
                            nxt = pair_slice(x, g, k + 2, b) if k + 2 < QN else pair_slice(x, g + 1, k + 2 - QN, b)
                            sp.dma_start(zx[:, k % 2, b, :, :], nxt).then_inc(zx_in[k % 2], 16)

            with sp.Fori(0, G - 1) as g:
                group(g, True)
            group(G - 1, False)
            sp.wait_ge(out_st, 32 * QN * G)
            sp.nop()

        @block.tensor
        def _(pe):
            pe.wait_ge(const_done, 3)
            for m in range(3):
                pe.wait_ge(abs_done, m + 1)
                nc.tensor.matmul(side[:, 0, 2 * m:2 * m + 2], ones[:, :], asum[:, m, :], start=True, stop=True).then_inc(total_done, 1)
            for m in range(3):
                pe.wait_ge(tern_done, m + 1)
                for jj in range(NJ // 2):
                    n = 4 * m + jj
                    if n >= 6:
                        pe.wait_ge(wt_copied, n - 5)
                    bank = acc[:, (n % 6) // 3, n % 3, :].bitcast(F16)
                    for j in range(2):
                        for c in range(NC):
                            if m < 2:
                                src = tern[m][0:CH, :].rearrange("p (c j d) -> p c j d", c=NC, j=NJ)[:, c, 2 * jj + j, :]
                                dst = bank[:, HW * j + CH * c:HW * j + CH * (c + 1)]
                                last = nc.tensor.transpose(dst, src, ident16[0:CH, 0:CH])
                            else:
                                src = tern[m][:, 0:NJ * HW].rearrange("p (j d) -> p j d", j=NJ)[:, 2 * jj + j, CH * c:CH * (c + 1)]
                                dst = bank[0:CH, (NC * j + c) * DB:(NC * j + c + 1) * DB]
                                last = nc.tensor.transpose(dst, src, ident16[:, :])
                    last.then_inc(wt_mm, 1)

            pe.wait_ge(wt_copied, 12)
            pe.wait_ge(kslot_done, 3)

            def transpose_pair(q):
                for b in range(2):
                    for t in range(NT):
                        i = QN * b + q
                        last = nc.tensor.transpose(side[:, b, t * P:(t + 1) * P], xr[:, t, i * DB:(i + 1) * DB], ident[:, :])
                last.then_inc(tr_mm, 1)

            for q in range(QN):
                pe.wait_ge(ln_done, NT)
                if q:
                    pe.wait_ge(tr_sum, q)
                transpose_pair(q)

            def triple(half, w, rows, operands, k, first, stop_last):
                for q in range(QN):
                    for a, o, slot in products[k][q]:
                        for h in range(2):
                            last = nc.tensor.matmul(acc[0:rows, half, a, :], w(slot_of[slot]), operands(q, o, h),
                                                    start=first and q == 0 and h == 0,
                                                    stop=stop_last and q == QN - 1 and h == 1)
                return last

            def group(g, more):
                for u in range(NU):
                    c, k = divmod(u, QN)
                    if u == 0:
                        pe.wait_ge(x_ready, QN * g + QN)
                    for half, w, done in ((0, wg, gate_mm), (1, wu, up_mm)):
                        pe.wait_ge(acc_read[half], PER * g + u + 1)
                        triple(half, lambda s, w=w: w[:, s, CH * c:CH * (c + 1)], CH,
                               lambda q, o, h: xop[:, q, o, h, :], k, True, True).then_inc(done, 1)
                    if 2 <= u < 6:
                        m = u - 2
                        if m == 0:
                            pe.wait_ge(tab_in, 32)
                        if m < 2:
                            pe.wait_ge(out_done, QN * g + 1)
                        else:
                            pe.wait_ge(power_done, QN * g + m - 1)
                        for q in range(QN):
                            last = nc.tensor.matmul(side[:, m % 2, :], dft_sb[:, q, m * P:(m + 1) * P], xop[:, q, 2, 0, :],
                                                    start=q == 0, stop=q == QN - 1)
                        last.then_inc(dft_mm, 1)
                    if 6 <= u < 10:
                        t = u - 6
                        if t < 2:
                            pe.wait_ge(power_done, QN * g + QN)
                        else:
                            pe.wait_ge(bound_done, NT * g + t - 1)
                        for m in range(QN):
                            last = nc.tensor.matmul(side[:, t % 2, 0:256], pw[:, m, t * P:(t + 1) * P], lag_sb[:, m, :],
                                                    start=m == 0, stop=m == QN - 1)
                        last.then_inc(lag_mm, 1)

                def back(k):
                    pe.wait_ge(acc_read[k % 2], PER * g + NU + k // 2 + 2)
                    if more:
                        pe.wait_ge(tr_sum, QN * g + QN + k + 1)
                    elif k:
                        pe.wait_ge(out_done, QN * g + k + 1)
                    else:
                        pe.wait_ge(bound_done, NT * g + NT)
                    for b in range(2):
                        for t in range(NT):
                            last = nc.tensor.transpose(side[:, b, t * P:(t + 1) * P], yt[:, b, t * P:(t + 1) * P], ident[:, :])
                    last.then_inc(back_mm, 1)

                for k in range(QN):
                    pe.wait_ge(acc_read[k % 2], PER * g + NU + k // 2 + 1)
                    for c in range(NC):
                        if k == 0:
                            pe.wait_ge(h_ready, NU * g + QN * (c + 1) + 1)
                            if c == 0:
                                pe.wait_ge(down_ready, 1)
                        last = triple(k % 2, lambda s: wd[:, s, c, :], P, lambda q, o, h: hop[0:CH, c, q, o, h, :],
                                      k, c == 0, c == NC - 1)
                        if c == NC - 1:
                            last.then_inc(down_mm, 1)
                        if k and c == 0:
                            back(k - 1)
                    if more:
                        if k == 0:
                            pe.wait_ge(ln_done, NT * g + 2 * NT)
                            pe.wait_ge(bound_done, NT * g + NT)
                        else:
                            pe.wait_ge(out_done, QN * g + k + 1)
                        transpose_pair(k)
                back(QN - 1)

            with pe.Fori(0, G - 1) as g:
                group(g, True)
            group(G - 1, False)
            pe.wait_ge(flag_sum, 1)
            nc.tensor.matmul(side[:, 0, 0:1], ones[:, :], fs[:, :], start=True, stop=True).then_inc(flag_mm, 1)

        @block.scalar
        def _(act):
            for m, w in ((0, w_gate), (1, w_up)):
                dst = stage[m].rearrange("p (c j d) -> p c j d", c=NC, j=NJ)
                for c in range(NC):
                    n = min(CH, HB - CH * c)
                    act.dma_start(dst[0:n, c, :, :], w[:, CH * c:CH * c + n, :].rearrange("j o d -> o j d")).then_inc(w_in[m], 16)
            act.dma_start(stage[2][:, 0:NJ * HB].rearrange("p (j d) -> p j d", j=NJ), w_down.rearrange("j o d -> o j d")).then_inc(w_in[2], 16)

            def row_sum(n, t, first=False):
                act.wait_ge(x_in[t], 16 * (n + 1))
                if t:
                    act.wait_ge(sum_done, NT * n + t)
                elif not first:
                    act.wait_ge(var_done, NT * n)
                nc.scalar.activation(junk[:, :], xr[:, t, :], ACT.Copy, accum_out=sm[:, t:t + 1]).then_inc(sum_done, 1)

            def row_var(n, t):
                act.wait_ge(mean_done, n + 1)
                if t:
                    act.wait_ge(var_done, NT * n + t)
                else:
                    act.wait_ge(sum_done, NT * n + NT)
                nc.scalar.activation(junk[:, :], xr[:, t, :], ACT.Square, bias=nm[:, t:t + 1], accum_out=vr[:, t:t + 1]).then_inc(var_done, 1)

            def split_pair(base, q):
                act.wait_ge(tr_mm, base + q + 1)
                if q:
                    act.wait_ge(tr_sum, base + q)
                nc.scalar.activation(xop[:, q, 0, 0, :], side[:, 0, :], ACT.Copy, scale=XS)
                nc.scalar.activation(xs[:, :], side[:, 0, :], ACT.Copy, scale=XS)
                nc.scalar.activation(xop[:, q, 1, 0, :], side[:, 1, :], ACT.Copy, scale=XS).then_inc(tr_hi, 1)
                act.wait_ge(tr_sum, base + q + 1)
                nc.scalar.activation(xop[:, q, 2, 0, :], ss[:, :], ACT.Copy).then_inc(tr_sumhi, 1)

            for t in range(NT):
                row_sum(0, t, first=True)
            for t in range(NT):
                row_var(0, t)
            for n in range(12):
                m, jj = divmod(n, 4)
                act.wait_ge(wt_mm, n + 1)
                bank = acc[:, (n % 6) // 3, n % 3, :].bitcast(F16)
                rows, width = (P, HW) if m < 2 else (CH, NC * DB)
                nc.scalar.activation(wt[m][0:rows, 2 * width * jj:2 * width * (jj + 1)], bank[0:rows, 0:2 * width], ACT.Copy).then_inc(wt_copied, 1)
            for q in range(QN):
                split_pair(0, q)

            def group(g, more):
                for u in range(NU):
                    c, k = divmod(u, QN)
                    act.wait_ge(gate_mm, NU * g + u + 1)
                    act.wait_ge(acc1_read, PER * g + u + 1)
                    nc.scalar.activation(kb[0:CH, :], acc[0:CH, 0, 0, :], ACT.Copy).then_inc(k_copied, 1)
                    act.wait_ge(acc0_read, PER * g + u + 2)
                    nc.scalar.activation(gb[:, :, :], gb[:, :, :], ACT.Silu, scale=gsc[0:CH, :]).then_inc(silu_done, 1)
                    act.wait_ge(up_mm, NU * g + u + 1)
                    nc.scalar.activation(kb[0:CH, :], acc[0:CH, 1, 0, :], ACT.Copy).then_inc(k_copied, 1)
                    act.wait_ge(h_sum, NU * g + u + 1)
                    nc.scalar.activation(hop[0:CH, c, k, :, 0, :], hh[:, :, :], ACT.Copy).then_inc(h_hi, 1)
                    if 2 <= u < 6:
                        m = u - 2
                        act.wait_ge(dft_mm, QN * g + m + 1)
                        nc.scalar.activation(pw[:, m, :], side[:, m % 2, :], ACT.Square, scale=1.0 / (8.0 * XS)).then_inc(power_done, 1)
                        if more:
                            row_sum(g + 1, m)
                    if more and 7 <= u < 11:
                        row_var(g + 1, u - 7)
                for k in range(QN):
                    act.wait_ge(down_mm, QN * g + k + 1)
                    act.wait_ge(acc_read[(k + 1) % 2], PER * g + NU + (k + 1) // 2 + 1)
                    nc.scalar.activation(kb[:, :], acc[:, k % 2, 0, :], ACT.Copy).then_inc(k_copied, 1)
                    if more:
                        split_pair(QN * g + QN, k)

            with act.Fori(0, G - 1) as g:
                group(g, True)
            group(G - 1, False)

            act.wait_ge(flag_done, 1)
            rows_left = act.value_load(flag[0:1, 0:1])
            with act.If(rows_left > 0):
                act.wait_ge(out_st, 32 * QN * G)
                with act.Fori(0, ROWS // P) as n:
                    act.dma_start(slow_x[:, :], x[bass.ds(P * n, P), :]).then_inc(s_sem["x_in"], 16)
                    act.dma_start(slow_out[:, :], out[bass.ds(P * n, P), :]).then_inc(s_sem["x_in"], 16)
                    act.wait_ge(s_sem["ex_in"], n + 1)
                    nc.scalar.activation(slow_w[:, :], slow_corr[:, :], ACT.Exp, bias=slow_neg[:, :]).then_inc(s_sem["act"], 1)
                    act.wait_ge(s_sem["ob"], n + 1)
                    act.dma_start(out[bass.ds(P * n, P), :], slow_out[:, :]).then_inc(s_sem["st"], 16)
                    act.wait_ge(s_sem["st"], 16 * n + 16)
                    act.nop()
            act.nop()

        @block.vector
        def _(dve):
            count = [0]

            def link(ins):
                count[0] += 1
                ins.then_inc(chain, 1)
                dve.wait_ge(chain, count[0])

            nc.vector.memset(rmin[:, :], 3.0e38)
            nc.vector.memset(rh[:, :], 3.0e38)
            nc.vector.memset(mh[:, :], -0.5).then_inc(out_done, 1)
            link(nc.vector.memset(asum[:, :, :], 0.0))
            for m in range(2):
                link(nc.vector.memset(tern[m][0:CH, 2 * NJ * DB:3 * NJ * DB], 0.0))
            link(nc.vector.memset(tern[2][:, 0:NJ * HW].rearrange("p (j d) -> p j d", j=NJ)[:, :, HB:HW], 0.0))
            LAST = HB - 2 * CH
            parts = []
            for m in range(2):
                full, rest = slice(0, 2 * NJ * DB), slice(2 * NJ * DB, 3 * NJ * DB)
                parts.append([(stage[m][0:CH, full], tern[m][0:CH, full], wt[m][0:CH, full]),
                              (stage[m][0:LAST, rest], tern[m][0:LAST, rest], wt[m][0:LAST, rest])])
            three = lambda a, w: a.rearrange("p (j d) -> p j d", j=NJ)[:, :, 0:w]
            parts.append([(stage[2][:, 0:NJ * HB], three(tern[2][:, 0:NJ * HW], HB), wt[2][:, 0:NJ * HB])])

            def keep_stats(g):
                nc.vector.tensor_copy(nmd[:, :], nm[:, :])
                nc.vector.tensor_copy(rsd[:, :], rs[:, :]).then_inc(kept, 1)
                dve.wait_ge(kept, g + 1)

            def mean(n):
                dve.wait_ge(sum_done, NT * n + NT)
                nc.vector.tensor_scalar_mul(nm[:, :], sm[:, :], -1.0 / D).then_inc(mean_done, 1)

            def tiny(ins, at):
                ins.then_inc(v_done, 1)
                dve.wait_ge(v_done, at)

            def rstd(n):
                dve.wait_ge(var_done, NT * n + NT)
                nc.vector.tensor_scalar(vr[:, :], vr[:, :], 1.0 / D, EPS, ALU.mult, ALU.add).then_inc(v_done, 1)
                dve.wait_ge(guess_done, n + 1)
                tiny(nc.vector.tensor_tensor(rr[:, :], r0[:, :], r0[:, :], ALU.mult), 5 * n + 2)
                tiny(nc.vector.tensor_tensor(rr[:, :], rr[:, :], vr[:, :], ALU.mult), 5 * n + 3)
                tiny(nc.vector.tensor_scalar(rr[:, :], rr[:, :], -0.5, 1.5, ALU.mult, ALU.add), 5 * n + 4)
                tiny(nc.vector.tensor_tensor(rs[:, :], r0[:, :], rr[:, :], ALU.mult), 5 * n + 5)

            HT = 2 * NT + 1

            def half_turn(n, first=False):
                for t in range(NT):
                    dve.wait_ge(ln_done, NT * n + t + 1)
                    if t or not first:
                        dve.wait_ge(s_half, HT * n + 2 * t)
                    nc.vector.tensor_tensor(ss[:, :], xr[:, t, 0:T], xr[:, t, T:2 * T], ALU.subtract).then_inc(s_half, 1)
                    dve.wait_ge(s_half, HT * n + 2 * t + 1)
                    nc.vector.scalar_tensor_tensor(kjunk, ss[:, :], 1.0, ss[:, :], ALU.mult, ALU.mult,
                                                   accum_out=dh[:, t:t + 1]).then_inc(s_half, 1)
                dve.wait_ge(s_half, HT * n + 2 * NT)
                nc.vector.tensor_tensor(rh[:, :], rh[:, :], dh[:, :], ALU.min).then_inc(s_half, 1)

            kjunk = junk2[:, :]

            for m in range(3):
                dve.wait_ge(w_in[m], 16 * (3 if m < 2 else 1))
                for n, (src, _, _) in enumerate(parts[m]):
                    last = nc.vector.tensor_reduce(asum[0:src.shape[0], m, n:n + 1], src, AX.X, ALU.add, apply_absolute_value=True)
                last.then_inc(abs_done, 1)
            for m in range(3):
                dve.wait_ge(total_done, 3)
                link(nc.vector.tensor_reduce(tot[:, m:m + 1], side[:, 0, 2 * m:2 * m + 2], AX.X, ALU.add))
                link(nc.vector.tensor_scalar_mul(thr[:, m:m + 1], tot[:, m:m + 1], 0.5 / N_W))
                link(nc.vector.tensor_scalar_mul(nthr[:, m:m + 1], tot[:, m:m + 1], -0.5 / N_W))
                for src, _, neg in parts[m]:
                    link(nc.vector.tensor_scalar(neg, src, nthr[0:src.shape[0], m:m + 1], None, ALU.is_lt))
                for src, val, neg in parts[m]:
                    if m == 2:
                        src, neg = three(src, HB), three(neg, HB)
                    last = nc.vector.scalar_tensor_tensor(val, src, thr[0:src.shape[0], m:m + 1], neg, ALU.is_gt, ALU.subtract)
                last.then_inc(tern_done, 1)
                if m == 0:
                    mean(0)
                    rstd(0)
            link(nc.vector.tensor_scalar_mul(gsc[:, :], thr[:, 0:1], 2.0 / XS))
            link(nc.vector.reciprocal(osc[:, :], thr[:, 0:1]))
            link(nc.vector.tensor_scalar_mul(hsc[:, :], osc[:, :], 0.5 * HS / XS))
            link(nc.vector.tensor_scalar(osc[:, :], thr[:, 0:1], thr[:, 1:2], 8.0 / HS, ALU.mult, ALU.mult))
            link(nc.vector.tensor_tensor(osc[:, :], osc[:, :], thr[:, 2:3], ALU.mult))

            def weight_sums(m):
                dve.wait_ge(wt_copied, 4 * m + 4)
                rows, width = (P, HW) if m < 2 else (CH, NC * DB)
                for n, (p, ca, cb) in enumerate(slots):
                    if ca and cb:
                        part = lambda j: wt[m][0:rows, width * j:width * (j + 1)]
                        dst = (wg[:, n, :], wu[:, n, :], wd[:, n, :, :].rearrange("p c d -> p (c d)"))[m]
                        if ca == cb == -1:
                            last = nc.vector.scalar_tensor_tensor(dst, part(p), -1.0, part(p + 4), ALU.mult, ALU.subtract)
                        elif ca == 1:
                            last = nc.vector.tensor_tensor(dst, part(p), part(p + 4), ALU.add if cb == 1 else ALU.subtract)
                        else:
                            last = nc.vector.tensor_tensor(dst, part(p + 4), part(p), ALU.subtract)
                return last

            def split_pair(base, q):
                dve.wait_ge(tr_hi, base + q + 1)
                for b in range(2):
                    nc.vector.scalar_tensor_tensor(xop[:, q, b, 1, :], side[:, b, :], XS, xop[:, q, b, 0, :], ALU.mult, ALU.subtract)
                if q:
                    dve.wait_ge(x_ready, base + q)
                nc.vector.scalar_tensor_tensor(ss[:, :], side[:, 1, :], XS, xs[:, :], ALU.mult, ALU.add).then_inc(tr_sum, 1)

            for m, done in ((0, acc0_read), (1, acc1_read), (2, down_ready)):
                weight_sums(m).then_inc(done, 1)
            half_turn(0, first=True)
            for q in range(QN):
                split_pair(0, q)

            def out_of_k(rows, half, k, dst):
                nc.vector.tensor_tensor(dst[:, 0, :], acc[0:rows, half, 1, :], kb[0:rows, :], ALU.add)
                return nc.vector.tensor_tensor(dst[:, 1, :], acc[0:rows, half, 2, :], kb[0:rows, :],
                                               ALU.add if DELTA[k] == 1 else ALU.subtract)

            def group(g, more):
                for u in range(NU):
                    c, k = divmod(u, QN)
                    dve.wait_ge(k_copied, (2 * NU + QN) * g + 2 * u + 1)
                    out_of_k(CH, 0, k, gb).then_inc(acc0_read, 1)
                    dve.wait_ge(k_copied, (2 * NU + QN) * g + 2 * u + 2)
                    dve.wait_ge(h_ready, NU * g + u + 1)
                    out_of_k(CH, 1, k, hh).then_inc(acc1_read, 1)
                    dve.wait_ge(silu_done, NU * g + u + 1)
                    dve.wait_ge(acc1_read, PER * g + u + 2)
                    nc.vector.scalar_tensor_tensor(hh[:, 0:2, :], gb[:, :, :], hsc[0:CH, :], hh[:, 0:2, :], ALU.mult, ALU.mult).then_inc(h_done, 1)
                    if u == 6:
                        keep_stats(g)
                        if more:
                            mean(g + 1)
                    if 6 <= u < 10:
                        dve.wait_ge(lag_mm, NT * g + u - 5)
                        nc.vector.tensor_reduce(dmin[:, u - 6:u - 5], side[:, u % 2, 0:256], AX.X, ALU.min).then_inc(bound_done, 1)
                dve.wait_ge(bound_done, NT * g + NT)
                nc.vector.tensor_tensor(rmin[:, :], rmin[:, :], dmin[:, :], ALU.min).then_inc(least_done, 1)
                dve.wait_ge(least_done, g + 1)
                if more:
                    rstd(g + 1)
                    half_turn(g + 1)
                for k in range(QN):
                    if k:
                        finish(g, k - 1)
                    if k == 0:
                        dve.wait_ge(lag_mm, NT * g + NT)
                    else:
                        dve.wait_ge(back_mm, QN * g + k)
                    dve.wait_ge(k_copied, (2 * NU + QN) * g + 2 * NU + k + 1)
                    out_of_k(P, k % 2, k, yt).then_inc(acc_read[k % 2], 1)
                    if more:
                        split_pair(QN * g + QN, k)
                finish(g, QN - 1)

            def finish(g, k):
                dve.wait_ge(z_done, QN * g + k + 1)
                dve.wait_ge(back_mm, QN * g + k + 1)
                z = zx[:, k % 2, :, :, :].rearrange("p b t c -> p (b t c)")
                nc.vector.scalar_tensor_tensor(z, side[:, :, :].rearrange("p b t -> p (b t)"), osc[:, :], z,
                                               ALU.mult, ALU.add).then_inc(out_done, 1)

            with dve.Fori(0, G - 1) as g:
                group(g, True)
            group(G - 1, False)

            link(nc.vector.tensor_scalar(fl[:, 0, :], rmin[:, :], MARGIN * LAG_SCALE, None, ALU.is_lt))
            link(nc.vector.tensor_scalar(fl[:, 1, :], rh[:, :], MARGIN, None, ALU.is_lt))
            nc.vector.tensor_reduce(fs[:, :], fl[:, :, :].rearrange("p a t -> p (a t)"), AX.X, ALU.add).then_inc(flag_sum, 1)
            dve.wait_ge(flag_mm, 1)
            nc.vector.tensor_copy(flag[:, :], side[:, 0, 0:1]).then_inc(flag_done, 1)
            dve.wait_ge(flag_done, 1)
            rows_left = dve.value_load(flag[0:1, 0:1])
            with dve.If(rows_left > 0):
                with dve.Fori(0, ROWS // P) as n:
                    step = [0]

                    def then(ins):
                        step[0] += 1
                        ins.then_inc(s_sem["dve"], 1)
                        dve.wait_ge(s_sem["dve"], STEPS * n + step[0])
                        dve.sem_inc(dve_tick, 1)

                    col = lambda i: slow_st[:, i:i + 1]
                    xx = slow_xx[:, 0:D]
                    dve.wait_ge(s_sem["x_in"], 32 * n + 32)
                    then(nc.vector.tensor_reduce(col(0), slow_x, AX.X, ALU.add))
                    then(nc.vector.tensor_scalar_mul(col(1), col(0), 1.0 / D))
                    then(nc.vector.tensor_scalar(slow_acc, slow_x, col(1), None, ALU.subtract))
                    then(nc.vector.scalar_tensor_tensor(slow_junk, slow_acc, 1.0, slow_acc, ALU.mult, ALU.mult, accum_out=col(2)))
                    then(nc.vector.tensor_scalar(col(3), col(2), 1.0 / D, EPS, ALU.mult, ALU.add))
                    then(nc.vector.tensor_scalar(col(5).bitcast(I32), col(3).bitcast(I32), 1, None, ALU.arith_shift_right))
                    then(nc.vector.tensor_copy(col(6), col(5).bitcast(I32)))
                    then(nc.vector.tensor_scalar(col(6), col(6), -1.0, float(0x5F3759DF), ALU.mult, ALU.add))
                    then(nc.vector.tensor_copy(col(5).bitcast(I32), col(6)))
                    for _ in range(4):
                        then(nc.vector.tensor_tensor(col(6), col(5), col(5), ALU.mult))
                        then(nc.vector.tensor_tensor(col(6), col(6), col(3), ALU.mult))
                        then(nc.vector.tensor_scalar(col(6), col(6), -0.5, 1.5, ALU.mult, ALU.add))
                        then(nc.vector.tensor_tensor(col(5), col(5), col(6), ALU.mult))
                    then(nc.vector.tensor_scalar(xx, slow_acc, col(5), None, ALU.mult))
                    then(nc.vector.tensor_copy(slow_xx[:, D:2 * D], xx))
                    with dve.Fori(0, D) as d:
                        nc.vector.tensor_tensor(slow_junk, xx, slow_xx[:, bass.ds(d, D)], ALU.mult).then_inc(s_lag, 1)
                        dve.wait_ge(s_lag, D * 2 * n + 2 * d + 1)
                        nc.vector.tensor_reduce(slow_corr[:, bass.ds(d, 1)], slow_junk, AX.X, ALU.add).then_inc(s_lag, 1)
                        dve.nop()
                    dve.wait_ge(s_lag, D * 2 * n + 2 * D)
                    dve.sem_inc(dve_tick, 1)
                    then(nc.vector.max(slow_top, slow_corr))
                    then(nc.vector.tensor_scalar_mul(slow_neg, slow_top[:, 0:1], -1.0))
                    then(nc.vector.memset(slow_top[:, TOP:8], 3.0e38))
                    then(nc.vector.match_replace(slow_mask, slow_top, slow_corr, -3.0e38))
                    nc.vector.tensor_scalar(slow_mask, slow_mask, -3.0e38, None, ALU.is_equal).then_inc(s_sem["ex_in"], 1)
                    dve.wait_ge(s_sem["act"], n + 1)
                    dve.wait_ge(s_sem["ex_in"], n + 1)
                    then(nc.vector.scalar_tensor_tensor(slow_w, slow_w, 1.0, slow_mask, ALU.mult, ALU.mult, accum_out=col(7)))
                    then(nc.vector.reciprocal(col(8), col(7)))
                    then(nc.vector.tensor_scalar(slow_w, slow_w, col(8), None, ALU.mult))
                    then(nc.vector.tensor_scalar(slow_acc, xx, -1.0, None, ALU.mult))
                    with dve.Fori(0, D) as d:
                        nc.vector.tensor_scalar(slow_junk, slow_xx[:, bass.ds(d, D)], slow_w[:, bass.ds(d, 1)], None, ALU.mult).then_inc(s_add, 1)
                        dve.wait_ge(s_add, D * 2 * n + 2 * d + 1)
                        nc.vector.tensor_tensor(slow_acc, slow_acc, slow_junk, ALU.add).then_inc(s_add, 1)
                        dve.wait_ge(s_add, D * 2 * n + 2 * d + 2)
                        dve.nop()
                    nc.vector.tensor_tensor(slow_out, slow_out, slow_acc, ALU.add).then_inc(s_sem["ob"], 1)
                    dve.nop()
            dve.nop()

        @block.gpsimd
        def _(pool):
            nc.gpsimd.memset(ident[:, :], 0.0).then_inc(pchain, 1)
            nc.gpsimd.memset(ident16[:, :], 0.0).then_inc(pchain, 1)
            nc.gpsimd.memset(ones[:, :], 1.0).then_inc(const_done, 1)
            pool.wait_ge(pchain, 2)
            for m in (ident, ident16):
                nc.gpsimd.affine_select(out=m[:, :], in_=m[:, :], compare_op=ALU.not_equal, fill=1.0, base=0,
                                        pattern=[[-1, P]], channel_multiplier=1).then_inc(const_done, 1)

            def normalise(n, base):
                pool.wait_ge(v_done, 5 * n + 1)
                nc.gpsimd.tensor_tensor(r0[:, :], vr[:, :], mh[:, :], ALU.pow).then_inc(guess_done, 1)
                pool.wait_ge(v_done, 5 * n + 5)
                pool.sem_inc(pool_tick, 1)
                for t in range(NT):
                    nc.gpsimd.tensor_scalar(xr[:, t, :], xr[:, t, :], nm[:, t:t + 1], rs[:, t:t + 1], ALU.add, ALU.mult).then_inc(ln_done, 1)

            def split_pair(base, q):
                pool.wait_ge(tr_sumhi, base + q + 1)
                nc.gpsimd.tensor_tensor(xop[:, q, 2, 1, :], ss[:, :], xop[:, q, 2, 0, :], ALU.subtract).then_inc(x_ready, 1)

            normalise(0, 0)
            for m in range(3):
                pool.wait_ge(wt_copied, 4 * m + 4)
                rows, width = (P, HW) if m < 2 else (CH, NC * DB)
                for n, (p, ca, cb) in enumerate(slots):
                    if not (ca and cb):
                        j = p if ca else p + 4
                        dst = (wg[:, n, :], wu[:, n, :], wd[:, n, :, :].rearrange("p c d -> p (c d)"))[m]
                        last = nc.gpsimd.tensor_scalar(dst, wt[m][0:rows, width * j:width * (j + 1)], float(ca + cb), None, ALU.mult)
                last.then_inc(kslot_done, 1)
            for q in range(QN):
                split_pair(0, q)
            nc.gpsimd.memset(pz[:, :], 0.0).then_inc(h_ready, 1)

            def group(g, more):
                for u in range(NU):
                    c, k = divmod(u, QN)
                    pool.wait_ge(h_done, NU * g + u + 1)
                    nc.gpsimd.tensor_tensor(hh[:, 2, :], hh[:, 0, :], hh[:, 1, :], ALU.add).then_inc(h_sum, 1)
                    pool.wait_ge(h_hi, NU * g + u + 1)
                    nc.gpsimd.tensor_tensor(hop[0:CH, c, k, :, 1, :], hh[:, :, :], hop[0:CH, c, k, :, 0, :], ALU.subtract).then_inc(h_ready, 1)
                if more:
                    normalise(g + 1, g + 1)
                for k in range(QN):
                    if k:
                        pool.wait_ge(z_done, QN * g + k)
                    pool.wait_ge(zx_in[k % 2], 32 * (QN // 2 * g + k // 2 + 1))
                    pool.sem_inc(pool_tick, 1)
                    for t in range(NT):
                        last = nc.gpsimd.tensor_scalar(zt[:, :, t, :], zx[:, k % 2, :, t, :], nmd[:, t:t + 1], rsd[:, t:t + 1], ALU.add, ALU.mult)
                    last.then_inc(z_part, 1)
                    pool.wait_ge(z_part, QN * g + k + 1)
                    nc.gpsimd.tensor_tensor(zx[:, k % 2, :, :, :].rearrange("p b t c -> p (b t c)"),
                                            zx[:, k % 2, :, :, :].rearrange("p b t c -> p (b t c)"),
                                            zt[:, :, :, :].rearrange("p b t c -> p (b t c)"), ALU.add).then_inc(z_done, 1)
                    if more:
                        split_pair(QN * g + QN, k)

            with pool.Fori(0, G - 1) as g:
                group(g, True)
            group(G - 1, False)


def kernel(L0_attn_x, L0_ffn_w_gate, L0_ffn_w_up, L0_ffn_w_down):
    import numpy as _np
    import concourse.bacc as _bacc
    from concourse import mybir as _mybir
    from concourse.bass_utils import run_bass_kernel_spmd as _run

    L, P = 1024, 128
    f = _np.arange(1, 257)[None, :]
    t = _np.arange(512)[:, None]
    angle = 2.0 * _np.pi * ((t * f) % 512) / 512.0
    dft = _np.concatenate([_np.cos(angle), _np.sin(angle)], axis=1).astype(_np.float16)
    dft = _np.ascontiguousarray(dft.reshape(4, P, 512).transpose(1, 0, 2))
    weight = _np.where(f == 256, 1.0, 2.0).reshape(256, 1)
    d = _np.arange(1, 257)[None, :]
    lag = weight * (1.0 - _np.cos(2.0 * _np.pi * ((f.reshape(256, 1) * d) % 512) / 512.0))
    lag = _np.concatenate([lag, lag], axis=0).astype(_np.float16)
    lag = _np.ascontiguousarray(lag.reshape(4, P, 256).transpose(1, 0, 2))

    arrays = {
        "in_x": _np.ascontiguousarray(_np.asarray(L0_attn_x)[0]),
        "in_w_gate": _np.ascontiguousarray(L0_ffn_w_gate),
        "in_w_up": _np.ascontiguousarray(L0_ffn_w_up),
        "in_w_down": _np.ascontiguousarray(L0_ffn_w_down),
        "in_dft": dft,
        "in_lag": lag,
    }
    nc = _bacc.Bacc("TRN2", target_bir_lowering=False, num_devices=1)
    args = [nc.dram_tensor(n, a.shape, _mybir.dt.from_np(a.dtype), kind="ExternalInput").ap() for n, a in arrays.items()]
    out = nc.dram_tensor("out_y", (2048, L), _mybir.dt.float32, kind="ExternalOutput").ap()
    octonion_ffn_attention_kernel(nc, *args, out)
    r = _run(nc, [arrays], core_ids=[0])
    return r.results[0]["out_y"].reshape(1, 2048, L)
```

```python
def octonion_ffn_attention_kernel(nc, x, w_gate, w_up, w_down, dft, lag, out):
    import concourse.bass as bass
    from concourse import mybir
    from contextlib import ExitStack

    F32, F16, I32 = mybir.dt.float32, mybir.dt.float16, mybir.dt.int32
    ALU, ACT, AX = mybir.AluOpType, mybir.ActivationFunctionType, mybir.AxisListType

    P = 128
    ROWS, D = x.shape
    NJ, HB, DB = w_gate.shape
    QN = NJ // 2
    NC = 3
    CH = -(-HB // NC)
    HW = NC * CH
    HP = (NC - 1) * CH + P
    T = 512
    NT = T // P
    G = ROWS // T
    NU = NC * QN
    N_W = NJ * HB * DB
    EPS = 1e-5
    XS = 1024.0
    HS = 2.0 ** -6
    MARGIN = 150.0
    LAG_SCALE = 16.0
    NL = 256
    LAGS = lag.shape[2]
    TOP = 6
    STEPS = 35
    DELTA = (1, -1, -1, 1)

    sign = [[0] * NJ for _ in range(NJ)]
    for i in range(NJ):
        sign[0][i] = sign[i][0] = 1
        if i:
            sign[i][i] = -1
    for a, b, c in [(1, 2, 3), (1, 4, 5), (1, 7, 6), (2, 4, 6), (2, 5, 7), (3, 4, 7), (3, 6, 5)]:
        for u, v in ((a, b), (b, c), (c, a)):
            sign[u][v], sign[v][u] = 1, -1
    products = []
    for k in range(QN):
        of_k = []
        for q in range(QN):
            p = k ^ q
            a, b, c, d = sign[p][q], sign[p + 4][q + 4], sign[p + 4][q], sign[p][q + 4]
            if a * d == DELTA[k]:
                of_k.append([(0, 2, (p, a, 0)), (1, 1, (p, -a, b)), (2, 0, (p, -d, c))])
            else:
                of_k.append([(0, 2, (p, 0, b)), (1, 0, (p, a, -b)), (2, 1, (p, d, -c))])
        products.append(of_k)
    slots = sorted({w for of_k in products for of_q in of_k for _, _, w in of_q})
    slot_of = {w: n for n, w in enumerate(slots)}
    NS = len(slots)

    ctx = ExitStack()
    with ctx:
        def sb(name, shape, dt):
            return ctx.enter_context(nc.sbuf_tensor(name, shape, dt))

        def sem(name):
            return ctx.enter_context(nc.semaphore(name))

        wg = sb("wg", [P, NS, HP], F16)
        wu = sb("wu", [P, NS, HP], F16)
        wd = sb("wd", [CH, NS, NC, DB], F16)
        xop = sb("xop", [P, QN, 3, 2, T], F16)
        hop = sb("hop", [P, NC, QN, 3, 2, T], F16)
        xr = sb("xr", [P, NT, D], F32)
        zx = sb("zx", [P, 2, 2, NT, DB], F32)
        zt = sb("zt", [P, 2, NT, DB], F32)
        kb = sb("kb", [P, T], F32)
        gb = sb("gb", [CH, 2, T], F32)
        hh = sb("hh", [CH, 3, T], F32)
        yt = sb("yt", [P, 2, T], F32)
        pw = yt[:, :, :].bitcast(F16).rearrange("p b (m t) -> p (b m) t", t=T)
        xs = sb("xs", [P, 2, T], F32)
        ss = sb("ss", [P, 2, T], F32)
        junk = zt[:, :, :, :].rearrange("p b t c -> p (b t c)")
        dft_sb = sb("dft_sb", [P, QN, T], F16)
        lag_sb = sb("lag_sb", [P, QN, LAGS], F16)
        ident = sb("ident", [P, P], F32)
        ident16 = sb("ident16", [P, P], F16)
        ones = sb("ones", [P, P], F32)
        asum = sb("asum", [P, 3, 2], F32)
        tot = sb("tot", [P, 3], F32)
        thr = sb("thr", [P, 3], F32)
        nthr = sb("nthr", [P, 3], F32)
        gsc = sb("gsc", [P, 1], F32)
        hsc = sb("hsc", [P, 1], F32)
        osc = sb("osc", [P, 1], F32)
        sm = sb("sm", [P, NT], F32)
        nm = sb("nm", [P, NT], F32)
        vr = sb("vr", [P, NT], F32)
        r0 = sb("r0", [P, NT], F32)
        rr = sb("rr", [P, NT], F32)
        rs = sb("rs", [P, NT], F32)
        nmd = sb("nmd", [P, NT], F32)
        rsd = sb("rsd", [P, NT], F32)
        mh = sb("mh", [P, NT], F32)
        dmin = sb("dmin", [P, NT], F32)
        rmin = sb("rmin", [P, NT], F32)
        un = sb("un", [P, NT], F32)
        hb = sb("hb", [P, NT], F32)
        fl = sb("fl", [P, NT], F32)
        fs = sb("fs", [P, 1], F32)
        flag = sb("flag", [P, 1], I32)
        pz = sb("pz", [P, 1], F32)

        prep = hop[:, :, :, :, :, :].rearrange("p c k o h t -> p (c k o h t)")
        stage, tern, wt = [], [], []
        for m in range(3):
            stage.append(prep[:, 6144 * m:6144 * (m + 1)].bitcast(F32))
            tern.append(prep[:, 18432 + 3072 * m:18432 + 3072 * (m + 1)])
            wt.append(prep[:, 27648 + 3072 * m:27648 + 3072 * (m + 1)])

        slow = prep.bitcast(F32)
        slow_x = slow[:, 0:D]
        slow_out = slow[:, D:2 * D]
        slow_corr = slow[:, 2 * D:3 * D]
        slow_w = slow[:, 3 * D:4 * D]
        slow_xx = slow[:, 4 * D:6 * D]
        slow_acc = slow[:, 6 * D:7 * D]
        slow_junk = slow[:, 7 * D:8 * D]
        slow_mask = slow[:, 8 * D:9 * D]
        slow_top = slow[:, 9 * D:9 * D + 8]
        slow_neg = slow[:, 9 * D + 8:9 * D + 9]
        slow_st = slow[:, 9 * D + 16:9 * D + 32]

        acc = ctx.enter_context(nc.psum_tensor("acc", [P, 2, 3, T], F32))
        side = ctx.enter_context(nc.psum_tensor("side", [P, 2, T], F32))

        first_banks = (side, acc[:, 1, 1:3, :])

        def weight_bank(n):
            if n >= NJ:
                return side[:, n % 2, :].bitcast(F16)
            return acc[:, n % 4 // 3, n % 4 % 3, :].bitcast(F16)

        def total_bank(m):
            return side[:, m % 2, 0:2]

        x_in = [sem(f"x_in{t}") for t in range(NT)]; w_in = [sem(f"w_in{m}") for m in range(3)]; tab_in = sem("tab_in"); zx_in = [sem(f"zx_in{n}") for n in range(2)]
        const_done = sem("const_done"); abs_done = [sem(f"abs_done{m}") for m in range(3)]; total_done = [sem(f"total_done{m}") for m in range(3)]
        total_read = sem("total_read"); tern_done = sem("tern_done"); wt_mm = sem("wt_mm"); wt_copied = sem("wt_copied")
        down_ready = sem("down_ready"); slots_ready = sem("slots_ready")
        sum_done = sem("sum_done"); mean_done = sem("mean_done"); var_done = sem("var_done"); v_done = sem("v_done")
        guess_done = sem("guess_done"); ln_done = sem("ln_done")
        tr_mm = sem("tr_mm"); tr_hi = sem("tr_hi"); xs_done = sem("xs_done"); ss_done = sem("ss_done"); tr_sum = sem("tr_sum"); tr_sumhi = sem("tr_sumhi"); x_ready = sem("x_ready")
        gate_mm = sem("gate_mm"); up_mm = sem("up_mm"); down_mm = sem("down_mm"); k_copied = sem("k_copied")
        acc0_read = sem("acc0_read"); acc1_read = sem("acc1_read"); silu_done = sem("silu_done"); h_done = sem("h_done")
        h_sum = sem("h_sum"); h_hi = sem("h_hi"); h_ready = sem("h_ready")
        dft_mm = sem("dft_mm"); power_done = sem("power_done"); lag_mm = sem("lag_mm"); bound_done = sem("bound_done")
        back_mm = sem("back_mm"); z_done = sem("z_done"); out_done = sem("out_done"); out_st = sem("out_st")
        chain = sem("chain"); pchain = sem("pchain"); flag_sum = sem("flag_sum"); flag_mm = sem("flag_mm"); flag_done = sem("flag_done")
        s_sem = {n: sem("slow_" + n) for n in ("x_in", "ex_in", "dve", "act", "st", "ob")}
        pool_tick = sem("pool_tick"); dve_tick = sem("dve_tick")
        kept = sem("kept")
        zeroed = sem("zeroed")
        least_done = sem("least_done")
        z_part = sem("z_part")
        s_lag = sem("slow_lag"); s_add = sem("slow_add")
        acc_read = (acc0_read, acc1_read)
        PER = NU + 2

        x_rows = x.rearrange("(n p) d -> n p d", p=P)
        out_rows = out.rearrange("(n p) d -> n p d", p=P)
        block = ctx.enter_context(nc.Block())

        def pair_slice(ap, g, k, b):
            return ap[bass.ds(T * g, T), (QN * b + k) * DB:(QN * b + k + 1) * DB].rearrange("(t p) c -> p t c", p=P)

        last_rows = HB - (NC - 1) * CH
        three = lambda a, w: a.rearrange("p (j d) -> p j d", j=NJ)[:, :, 0:w]
        parts = []
        for m in range(2):
            full, rest = slice(0, 2 * NJ * DB), slice(2 * NJ * DB, 3 * NJ * DB)
            parts.append([(stage[m][0:CH, full], tern[m][0:CH, full], wt[m][0:CH, full]),
                          (stage[m][0:last_rows, rest], tern[m][0:last_rows, rest], wt[m][0:last_rows, rest])])
        parts.append([(stage[2][:, 0:NJ * HB], three(tern[2][:, 0:NJ * HW], HB), wt[2][:, 0:NJ * HB])])

        @block.sync
        def _(sp):
            sp.wait_ge(w_in[0], 48)
            for t in range(NT):
                sp.dma_start(xr[:, t, :], x_rows[t, :, :]).then_inc(x_in[t], 16)
            sp.wait_ge(w_in[1], 48)
            sp.dma_start(stage[2][:, 0:NJ * HB].rearrange("p (j d) -> p j d", j=NJ), w_down.rearrange("j o d -> o j d")).then_inc(w_in[2], 16)
            for k in range(2):
                for b in range(2):
                    sp.dma_start(zx[:, k, b, :, :], pair_slice(x, 0, k, b)).then_inc(zx_in[k], 16)
            sp.dma_start(dft_sb[:, :, :], dft).then_inc(tab_in, 16)
            sp.dma_start(lag_sb[:, :, :], lag).then_inc(tab_in, 16)

            def group(g, more):
                if more:
                    sp.wait_ge(tr_mm, QN * g + QN)
                    for t in range(NT):
                        sp.dma_start(xr[:, t, :], x[bass.ds(T * g + T + P * t, P), :]).then_inc(x_in[t], 16)
                for k in range(QN):
                    sp.wait_ge(out_done, QN * g + k + 2)
                    for b in range(2):
                        sp.dma_start(pair_slice(out, g, k, b), zx[:, k % 2, b, :, :]).then_inc(out_st, 16)
                    if k + 2 < QN or more:
                        sp.wait_ge(out_st, 32 * (QN * g + k + 1))
                        for b in range(2):
                            nxt = pair_slice(x, g, k + 2, b) if k + 2 < QN else pair_slice(x, g + 1, k + 2 - QN, b)
                            sp.dma_start(zx[:, k % 2, b, :, :], nxt).then_inc(zx_in[k % 2], 16)

            with sp.Fori(0, G - 1) as g:
                group(g, True)
            group(G - 1, False)
            sp.wait_ge(out_st, 32 * QN * G)
            sp.nop()

        @block.tensor
        def _(pe):
            pe.wait_ge(const_done, 3)

            def total(m):
                pe.wait_ge(abs_done[m], 1)
                nc.tensor.matmul(total_bank(m), ones[:, :], asum[:, m, :], start=True, stop=True).then_inc(total_done[m], 1)

            def transpose_weights(m, bankfuls=range(NJ // 2)):
                pe.wait_ge(tern_done, m + 1)
                for jj in bankfuls:
                    n = NJ // 2 * m + jj
                    if 4 <= n < NJ or n >= NJ + 2:
                        pe.wait_ge(wt_copied, n - 3 if n < NJ else n - 1)
                    bank = weight_bank(n)
                    for j in range(2):
                        for c in range(NC):
                            if m < 2:
                                src = tern[m][0:CH, :].rearrange("p (c j d) -> p c j d", c=NC, j=NJ)[:, c, 2 * jj + j, :]
                                dst = bank[:, HW * j + CH * c:HW * j + CH * (c + 1)]
                                last = nc.tensor.transpose(dst, src, ident16[0:CH, 0:CH])
                            else:
                                src = tern[m][:, 0:NJ * HW].rearrange("p (j d) -> p j d", j=NJ)[:, 2 * jj + j, CH * c:CH * (c + 1)]
                                dst = bank[0:CH, (NC * j + c) * DB:(NC * j + c + 1) * DB]
                                last = nc.tensor.transpose(dst, src, ident16[:, :])
                    last.then_inc(wt_mm, 1)

            def transpose_pair(q, banks):
                for b in range(2):
                    for t in range(NT):
                        i = QN * b + q
                        last = nc.tensor.transpose(banks[:, b, t * P:(t + 1) * P], xr[:, t, i * DB:(i + 1) * DB], ident[:, :])
                last.then_inc(tr_mm, 1)

            total(0)
            transpose_weights(0)
            total(1)
            transpose_weights(1)
            pe.wait_ge(ln_done, NT)
            for q in range(QN):
                if q == 0:
                    pe.wait_ge(total_read, 2)
                if q >= 2:
                    pe.wait_ge(tr_sum, q - 1)
                transpose_pair(q, first_banks[q % 2])
            pe.wait_ge(wt_copied, NJ)

            def triple(half, w, operands, k, first, last_chunk, before=lambda q: None):
                for q in range(QN):
                    before(q)
                    for a, o, slot in products[k][q]:
                        for h in range(2):
                            last = nc.tensor.matmul(acc[:, half, a, :], w(slot_of[slot]), operands(q, o, h),
                                                    start=first and q == 0 and h == 0,
                                                    stop=last_chunk and q == QN - 1 and h == 1)
                return last

            def gate_up(g, u):
                c, k = divmod(u, QN)

                def before(q):
                    if u == 0:
                        pe.wait_ge(tr_sum, QN * g + q + 1)
                        pe.wait_ge(x_ready, QN * g + q + 1)

                for half, w, done in ((0, wg, gate_mm), (1, wu, up_mm)):
                    pe.wait_ge(acc_read[half], PER * g + u + 1)
                    if u == QN:
                        pe.wait_ge(slots_ready, half + 1)
                    triple(half, lambda s, w=w: w[:, s, CH * c:CH * c + P], lambda q, o, h: xop[:, q, o, h, :],
                           k, True, True, before if half == 0 else lambda q: None).then_inc(done, 1)
                if 3 <= u < 7:
                    m = u - 3
                    if m == 0:
                        pe.wait_ge(tab_in, 32)
                        pe.wait_ge(wt_copied, 12)
                    if m < 2:
                        pe.wait_ge(out_done, QN * g + 1)
                    else:
                        pe.wait_ge(power_done, QN * g + m - 1)
                    for q in range(QN):
                        last = nc.tensor.matmul(side[:, m % 2, :], dft_sb[:, q, m * P:(m + 1) * P], xop[:, q, 2, 0, :],
                                                start=q == 0, stop=q == QN - 1)
                    last.then_inc(dft_mm, 1)
                if 7 <= u < 11:
                    t = u - 7
                    if t < 2:
                        pe.wait_ge(power_done, QN * g + QN)
                    else:
                        pe.wait_ge(bound_done, NT * g + t - 1)
                    for m in range(QN):
                        last = nc.tensor.matmul(side[:, t % 2, 0:LAGS], pw[:, m, t * P:(t + 1) * P], lag_sb[:, m, :],
                                                start=m == 0, stop=m == QN - 1)
                    last.then_inc(lag_mm, 1)

            def down(g, more):
                def back(k):
                    pe.wait_ge(acc_read[k % 2], PER * g + NU + k // 2 + 2)
                    if k == 0:
                        pe.wait_ge(bound_done, NT * g + NT)
                    elif more:
                        pe.wait_ge(tr_sum, QN * g + QN + k + 1)
                    else:
                        pe.wait_ge(out_done, QN * g + k + 1)
                    for b in range(2):
                        for t in range(NT):
                            last = nc.tensor.transpose(side[:, b, t * P:(t + 1) * P], yt[:, b, t * P:(t + 1) * P], ident[:, :])
                    last.then_inc(back_mm, 1)

                def next_pair(q):
                    if q == 0:
                        pe.wait_ge(ln_done, NT * g + 2 * NT)
                    if q == 1:
                        pe.wait_ge(tr_sum, QN * g + QN + 1)
                    else:
                        pe.wait_ge(out_done, QN * g + max(q, 1) + 1)
                    transpose_pair(q, side)

                if more:
                    between = {(1, 0): [(back, 0)], (1, 1): [(next_pair, 0)], (2, 0): [(next_pair, 1)], (2, 1): [(back, 1)],
                               (2, 2): [(next_pair, 2)], (3, 0): [(back, 2)], (3, 1): [(next_pair, 3)]}
                else:
                    between = {(k, 0): [(back, k - 1)] for k in range(1, QN)}
                for k in range(QN):
                    pe.wait_ge(acc_read[k % 2], PER * g + NU + k // 2 + 1)
                    for c in range(NC):
                        if k == 0:
                            pe.wait_ge(h_ready, NU * g + QN * (c + 1) + 1)
                            if c == 0:
                                pe.wait_ge(down_ready, 1)
                        last = triple(k % 2, lambda s: wd[:, s, c, :], lambda q, o, h: hop[0:CH, c, q, o, h, :],
                                      k, c == 0, c == NC - 1)
                        if c == NC - 1:
                            last.then_inc(down_mm, 1)
                        for step, n in between.get((k, c), []):
                            step(n)
                if more:
                    gate_up(g + 1, 0)
                back(QN - 1)

            def group(g, more):
                for u in range(QN, NU):
                    gate_up(g, u)
                down(g, more)
                if more:
                    for u in range(1, QN):
                        gate_up(g + 1, u)

            gate_up(0, 0)
            total(2)
            gate_up(0, 1)
            pe.wait_ge(total_read, 3)
            transpose_weights(2, (0, 1))
            gate_up(0, 2)
            transpose_weights(2, (2, 3))
            gate_up(0, 3)
            with pe.Fori(0, G - 1) as g:
                group(g, True)
            group(G - 1, False)
            pe.wait_ge(flag_sum, 1)
            nc.tensor.matmul(side[:, 0, 0:1], ones[:, :], fs[:, :], start=True, stop=True).then_inc(flag_mm, 1)

        @block.scalar
        def _(act):
            for m, w in ((0, w_gate), (1, w_up)):
                dst = stage[m].rearrange("p (c j d) -> p c j d", c=NC, j=NJ)
                for c in range(NC):
                    n = min(CH, HB - CH * c)
                    act.dma_start(dst[0:n, c, :, :], w[:, CH * c:CH * c + n, :].rearrange("j o d -> o j d")).then_inc(w_in[m], 16)

            def row_sum(n, t, first=False):
                act.wait_ge(x_in[t], 16 * (n + 1))
                if t:
                    act.wait_ge(sum_done, NT * n + t)
                elif not first:
                    act.wait_ge(var_done, NT * n)
                nc.scalar.activation(junk, xr[:, t, :], ACT.Copy, accum_out=sm[:, t:t + 1]).then_inc(sum_done, 1)

            def row_var(n, t):
                act.wait_ge(mean_done, n + 1)
                if t:
                    act.wait_ge(var_done, NT * n + t)
                else:
                    act.wait_ge(sum_done, NT * n + NT)
                nc.scalar.activation(junk, xr[:, t, :], ACT.Square, bias=nm[:, t:t + 1], accum_out=vr[:, t:t + 1]).then_inc(var_done, 1)

            def pair_heads(base, q, banks):
                act.wait_ge(tr_mm, base + q + 1)
                if q >= 2:
                    act.wait_ge(ss_done, base + q - 1)
                nc.scalar.activation(xop[:, q, 1, 0, :], banks[:, 1, :], ACT.Copy, scale=XS)
                nc.scalar.activation(xs[:, q % 2, :], banks[:, 0, :], ACT.Copy, scale=XS).then_inc(xs_done, 1)
                nc.scalar.activation(xop[:, q, 0, 0, :], banks[:, 0, :], ACT.Copy, scale=XS).then_inc(tr_hi, 1)

            def sum_head(base, q):
                act.wait_ge(ss_done, base + q + 1)
                nc.scalar.activation(xop[:, q, 2, 0, :], ss[:, q % 2, :], ACT.Copy).then_inc(tr_sumhi, 1)

            def absolute(m):
                act.wait_ge(w_in[m], 16 * (3 if m < 2 else 1))
                for n, (src, val, _) in enumerate(parts[m]):
                    if m == 2:
                        src = three(src, HB)
                    last = nc.scalar.activation(val, src, ACT.Abs, accum_out=asum[0:src.shape[0], m, n:n + 1])
                last.then_inc(abs_done[m], 1)

            def weights_out(m, bankfuls=range(NJ // 2)):
                for jj in bankfuls:
                    n = NJ // 2 * m + jj
                    act.wait_ge(wt_mm, n + 1)
                    rows, width = (P, HW) if m < 2 else (CH, NC * DB)
                    nc.scalar.activation(wt[m][0:rows, 2 * width * jj:2 * width * (jj + 1)], weight_bank(n)[0:rows, 0:2 * width], ACT.Copy).then_inc(wt_copied, 1)

            for t in range(NT):
                row_sum(0, t, first=True)
            act.wait_ge(zeroed, 1)
            absolute(1)
            for t in range(NT):
                row_var(0, t)
            weights_out(0)
            absolute(2)
            weights_out(1)
            pair_heads(0, 0, first_banks[0])
            pair_heads(0, 1, first_banks[1])
            for q in range(2, QN):
                sum_head(0, q - 2)
                pair_heads(0, q, first_banks[q % 2])
            sum_head(0, QN - 2)
            sum_head(0, QN - 1)

            def gate_up(g, u, more):
                c, k = divmod(u, QN)
                act.wait_ge(gate_mm, NU * g + u + 1)
                act.wait_ge(acc1_read, PER * g + u + 1)
                nc.scalar.activation(kb[0:CH, :], acc[0:CH, 0, 0, :], ACT.Copy).then_inc(k_copied, 1)
                act.wait_ge(acc0_read, PER * g + u + 2)
                nc.scalar.activation(gb[:, :, :], gb[:, :, :], ACT.Silu, scale=gsc[0:CH, :]).then_inc(silu_done, 1)
                act.wait_ge(up_mm, NU * g + u + 1)
                nc.scalar.activation(kb[0:CH, :], acc[0:CH, 1, 0, :], ACT.Copy).then_inc(k_copied, 1)
                act.wait_ge(h_sum, NU * g + u + 1)
                nc.scalar.activation(hop[0:CH, c, k, :, 0, :], hh[:, :, :], ACT.Copy).then_inc(h_hi, 1)
                if 3 <= u < 7:
                    m = u - 3
                    act.wait_ge(dft_mm, QN * g + m + 1)
                    nc.scalar.activation(pw[:, m, :], side[:, m % 2, :], ACT.Square, scale=1.0 / (8.0 * XS)).then_inc(power_done, 1)
                if more and 4 <= u < 6:
                    for t in range(2 * (u - 4), 2 * (u - 4) + 2):
                        row_sum(g + 1, t)
                if more and 7 <= u < 11:
                    row_var(g + 1, u - 7)

            def down(g, more):
                def k_out(k):
                    act.wait_ge(down_mm, QN * g + k + 1)
                    act.wait_ge(acc_read[(k + 1) % 2], PER * g + NU + (k + 1) // 2 + 1)
                    nc.scalar.activation(kb[:, :], acc[:, k % 2, 0, :], ACT.Copy).then_inc(k_copied, 1)

                def split(q):
                    pair_heads(QN * g + QN, q, side)
                    sum_head(QN * g + QN, q)

                if more:
                    steps = [(k_out, 0), (split, 0), (k_out, 1), (split, 1), (k_out, 2), (split, 2), (split, 3), (k_out, 3)]
                else:
                    steps = [(k_out, k) for k in range(QN)]
                for step, n in steps:
                    step(n)

            def group(g, more):
                for u in range(QN, NU):
                    gate_up(g, u, more)
                down(g, more)
                if more:
                    for u in range(QN):
                        gate_up(g + 1, u, True)

            gate_up(0, 0, True)
            gate_up(0, 1, True)
            weights_out(2, (0, 1))
            gate_up(0, 2, True)
            weights_out(2, (2, 3))
            gate_up(0, 3, True)
            with act.Fori(0, G - 1) as g:
                group(g, True)
            group(G - 1, False)

            act.wait_ge(flag_done, 1)
            rows_left = act.value_load(flag[0:1, 0:1])
            with act.If(rows_left > 0):
                act.wait_ge(out_st, 32 * QN * G)
                with act.Fori(0, ROWS // P) as n:
                    act.dma_start(slow_x[:, :], x[bass.ds(P * n, P), :]).then_inc(s_sem["x_in"], 16)
                    act.dma_start(slow_out[:, :], out[bass.ds(P * n, P), :]).then_inc(s_sem["x_in"], 16)
                    act.wait_ge(s_sem["ex_in"], n + 1)
                    nc.scalar.activation(slow_w[:, :], slow_corr[:, :], ACT.Exp, bias=slow_neg[:, :]).then_inc(s_sem["act"], 1)
                    act.wait_ge(s_sem["ob"], n + 1)
                    act.dma_start(out[bass.ds(P * n, P), :], slow_out[:, :]).then_inc(s_sem["st"], 16)
                    act.wait_ge(s_sem["st"], 16 * n + 16)
                    act.nop()
            act.nop()

        @block.vector
        def _(dve):
            count = [0]

            def link(ins):
                count[0] += 1
                ins.then_inc(chain, 1)
                dve.wait_ge(chain, count[0])

            nc.vector.memset(rmin[:, :], 3.0e38)
            for w in (wg, wu):
                nc.vector.memset(w[:, :, HW:HP], 0.0)
            nc.vector.memset(mh[:, :], -0.5).then_inc(out_done, 1)
            for m in range(2):
                nc.vector.memset(tern[m][0:CH, 2 * NJ * DB:3 * NJ * DB], 0.0)
            nc.vector.memset(tern[2][:, 0:NJ * HW].rearrange("p (j d) -> p j d", j=NJ)[:, :, HB:HW], 0.0)
            nc.vector.memset(asum[:, :, :], 0.0).then_inc(zeroed, 1)
            dve.wait_ge(zeroed, 1)

            def keep_stats(g):
                nc.vector.tensor_copy(nmd[:, :], nm[:, :])
                nc.vector.tensor_copy(rsd[:, :], rs[:, :]).then_inc(kept, 1)
                dve.wait_ge(kept, g + 1)

            def mean(n):
                dve.wait_ge(sum_done, NT * n + NT)
                nc.vector.tensor_scalar_mul(nm[:, :], sm[:, :], -1.0 / D).then_inc(mean_done, 1)

            def tiny(ins, at):
                ins.then_inc(v_done, 1)
                dve.wait_ge(v_done, at)

            def variance(n):
                dve.wait_ge(var_done, NT * n + NT)
                nc.vector.tensor_scalar(vr[:, :], vr[:, :], 1.0 / D, EPS, ALU.mult, ALU.add).then_inc(v_done, 1)

            def rstd(n):
                dve.wait_ge(guess_done, n + 1)
                tiny(nc.vector.tensor_tensor(rr[:, :], r0[:, :], r0[:, :], ALU.mult), 5 * n + 2)
                tiny(nc.vector.tensor_tensor(rr[:, :], rr[:, :], vr[:, :], ALU.mult), 5 * n + 3)
                tiny(nc.vector.tensor_scalar(rr[:, :], rr[:, :], -0.5, 1.5, ALU.mult, ALU.add), 5 * n + 4)
                tiny(nc.vector.tensor_tensor(rs[:, :], r0[:, :], rr[:, :], ALU.mult), 5 * n + 5)

            def thresholds(m):
                dve.wait_ge(total_done[m], 1)
                nc.vector.tensor_reduce(tot[:, m:m + 1], total_bank(m), AX.X, ALU.add).then_inc(total_read, 1)
                dve.wait_ge(total_read, m + 1)
                link(nc.vector.tensor_scalar_mul(thr[:, m:m + 1], tot[:, m:m + 1], 0.5 / N_W))
                link(nc.vector.tensor_scalar_mul(nthr[:, m:m + 1], tot[:, m:m + 1], -0.5 / N_W))

            def ternary(m):
                for src, _, neg in parts[m]:
                    link(nc.vector.tensor_scalar(neg, src, nthr[0:src.shape[0], m:m + 1], None, ALU.is_lt))
                for src, val, neg in parts[m]:
                    if m == 2:
                        src, neg = three(src, HB), three(neg, HB)
                    last = nc.vector.scalar_tensor_tensor(val, src, thr[0:src.shape[0], m:m + 1], neg, ALU.is_gt, ALU.subtract)
                last.then_inc(tern_done, 1)

            def weight_slots(m, lo, hi, ready):
                dve.wait_ge(wt_copied, NJ // 2 * (m + 1))
                rows, width = (P, HW) if m < 2 else (CH, NC * DB)
                part = lambda j: wt[m][0:rows, width * j + lo:width * j + hi]
                for n, (p, ca, cb) in enumerate(slots):
                    dst = (wg[:, n, :], wu[:, n, :], wd[:, n, :, :].rearrange("p c d -> p (c d)"))[m][:, lo:hi]
                    if not (ca and cb):
                        last = nc.vector.tensor_scalar_mul(dst, part(p if ca else p + 4), float(ca + cb))
                    elif ca == cb == -1:
                        last = nc.vector.scalar_tensor_tensor(dst, part(p), -1.0, part(p + 4), ALU.mult, ALU.subtract)
                    elif ca == 1:
                        last = nc.vector.tensor_tensor(dst, part(p), part(p + 4), ALU.add if cb == 1 else ALU.subtract)
                    else:
                        last = nc.vector.tensor_tensor(dst, part(p + 4), part(p), ALU.subtract)
                last.then_inc(ready, 1)

            def split_pair(base, q, banks):
                if q >= 2:
                    dve.wait_ge(x_ready, base + q - 1)
                dve.wait_ge(xs_done, base + q + 1)
                nc.vector.scalar_tensor_tensor(ss[:, q % 2, :], banks[:, 1, :], XS, xs[:, q % 2, :], ALU.mult, ALU.add).then_inc(ss_done, 1)
                for b in (1, 0):
                    if b == 0:
                        dve.wait_ge(tr_hi, base + q + 1)
                    last = nc.vector.scalar_tensor_tensor(xop[:, q, b, 1, :], banks[:, b, :], XS, xop[:, q, b, 0, :], ALU.mult, ALU.subtract)
                last.then_inc(tr_sum, 1)

            dve.wait_ge(w_in[0], 48)
            for n, (src, _, _) in enumerate(parts[0]):
                last = nc.vector.tensor_reduce(asum[0:src.shape[0], 0, n:n + 1], src, AX.X, ALU.add, apply_absolute_value=True)
            last.then_inc(abs_done[0], 1)
            thresholds(0)
            ternary(0)
            mean(0)
            thresholds(1)
            ternary(1)
            variance(0)
            rstd(0)
            for t in range(NT):
                nc.vector.tensor_scalar(xr[:, t, :], xr[:, t, :], nm[:, t:t + 1], rs[:, t:t + 1], ALU.add, ALU.mult).then_inc(ln_done, 1)
            weight_slots(0, 0, P, acc0_read)
            for q in range(QN):
                split_pair(0, q, first_banks[q % 2])
            weight_slots(1, 0, P, acc1_read)
            link(nc.vector.tensor_scalar_mul(gsc[:, :], thr[:, 0:1], 2.0 / XS))
            link(nc.vector.reciprocal(hsc[:, :], thr[:, 0:1]))
            link(nc.vector.tensor_scalar_mul(hsc[:, :], hsc[:, :], 0.5 * HS / XS))

            def out_of_k(rows, half, k, dst):
                nc.vector.tensor_tensor(dst[:, 0, :], acc[0:rows, half, 1, :], kb[0:rows, :], ALU.add)
                return nc.vector.tensor_tensor(dst[:, 1, :], acc[0:rows, half, 2, :], kb[0:rows, :],
                                               ALU.add if DELTA[k] == 1 else ALU.subtract)

            def least(g):
                def then(ins, n):
                    ins.then_inc(least_done, 1)
                    dve.wait_ge(least_done, 5 * g + n)
                then(nc.vector.tensor_tensor(hb[:, :], rsd[:, :], rsd[:, :], ALU.mult), 1)
                then(nc.vector.tensor_scalar(hb[:, :], hb[:, :], -2.0 * LAG_SCALE * D * EPS, 2.0 * LAG_SCALE * D, ALU.mult, ALU.add), 2)
                dve.wait_ge(bound_done, NT * g + NT)
                then(nc.vector.tensor_tensor(hb[:, :], hb[:, :], un[:, :], ALU.subtract), 3)
                then(nc.vector.tensor_tensor(hb[:, :], hb[:, :], dmin[:, :], ALU.min), 4)
                then(nc.vector.tensor_tensor(rmin[:, :], rmin[:, :], hb[:, :], ALU.min), 5)

            def gate_up(g, u, more):
                c, k = divmod(u, QN)
                dve.wait_ge(k_copied, (2 * NU + QN) * g + 2 * u + 1)
                out_of_k(CH, 0, k, gb).then_inc(acc0_read, 1)
                dve.wait_ge(k_copied, (2 * NU + QN) * g + 2 * u + 2)
                dve.wait_ge(h_ready, NU * g + u + 1)
                out_of_k(CH, 1, k, hh).then_inc(acc1_read, 1)
                dve.wait_ge(silu_done, NU * g + u + 1)
                dve.wait_ge(acc1_read, PER * g + u + 2)
                nc.vector.scalar_tensor_tensor(hh[:, 0:2, :], gb[:, :, :], hsc[0:CH, :], hh[:, 0:2, :], ALU.mult, ALU.mult).then_inc(h_done, 1)
                if u == 6:
                    keep_stats(g)
                    if more:
                        mean(g + 1)
                if 7 <= u < 11:
                    t = u - 7
                    dve.wait_ge(lag_mm, NT * g + t + 1)
                    nc.vector.tensor_copy(un[:, t:t + 1], side[:, t % 2, NL:NL + 1])
                    nc.vector.tensor_reduce(dmin[:, t:t + 1], side[:, t % 2, 0:NL], AX.X, ALU.min).then_inc(bound_done, 1)
                if u == 10 and more:
                    variance(g + 1)
                if u == 11:
                    least(g)
                    if more:
                        rstd(g + 1)

            def finish(g, k):
                dve.wait_ge(z_done, QN * g + k + 1)
                dve.wait_ge(back_mm, QN * g + k + 1)
                z = zx[:, k % 2, :, :, :].rearrange("p b t c -> p (b t c)")
                nc.vector.scalar_tensor_tensor(z, side[:, :, :].rearrange("p b t -> p (b t)"), osc[:, :], z,
                                               ALU.mult, ALU.add).then_inc(out_done, 1)

            def down(g, more):
                def down_y(k):
                    if k == 0:
                        dve.wait_ge(lag_mm, NT * g + NT)
                    else:
                        dve.wait_ge(back_mm, QN * g + k)
                    dve.wait_ge(k_copied, (2 * NU + QN) * g + 2 * NU + k + 1)
                    out_of_k(P, k % 2, k, yt).then_inc(acc_read[k % 2], 1)

                def split(q):
                    split_pair(QN * g + QN, q, side)

                def done(k):
                    finish(g, k)

                if more:
                    steps = [(down_y, 0), (done, 0), (split, 0), (down_y, 1), (split, 1), (done, 1), (down_y, 2), (split, 2),
                             (done, 2), (split, 3), (down_y, 3)]
                else:
                    steps = [(down_y, 0), (done, 0), (down_y, 1), (done, 1), (down_y, 2), (done, 2), (down_y, 3)]
                for step, n in steps:
                    step(n)

            def group(g, more):
                for u in range(QN, NU):
                    gate_up(g, u, more)
                down(g, more)
                if more:
                    gate_up(g + 1, 0, True)
                finish(g, QN - 1)
                if more:
                    for u in range(1, QN):
                        gate_up(g + 1, u, True)

            gate_up(0, 0, True)
            thresholds(2)
            link(nc.vector.tensor_scalar(osc[:, :], thr[:, 0:1], thr[:, 1:2], 8.0 / HS, ALU.mult, ALU.mult))
            link(nc.vector.tensor_tensor(osc[:, :], osc[:, :], thr[:, 2:3], ALU.mult))
            ternary(2)
            gate_up(0, 1, True)
            weight_slots(0, P, HW, slots_ready)
            gate_up(0, 2, True)
            weight_slots(1, P, HW, slots_ready)
            gate_up(0, 3, True)
            weight_slots(2, 0, NC * DB, down_ready)
            with dve.Fori(0, G - 1) as g:
                group(g, True)
            group(G - 1, False)

            link(nc.vector.tensor_scalar(fl[:, :], rmin[:, :], MARGIN * LAG_SCALE, None, ALU.is_lt))
            nc.vector.tensor_reduce(fs[:, :], fl[:, :], AX.X, ALU.add).then_inc(flag_sum, 1)
            dve.wait_ge(flag_mm, 1)
            nc.vector.tensor_copy(flag[:, :], side[:, 0, 0:1]).then_inc(flag_done, 1)
            dve.wait_ge(flag_done, 1)
            rows_left = dve.value_load(flag[0:1, 0:1])
            with dve.If(rows_left > 0):
                with dve.Fori(0, ROWS // P) as n:
                    step = [0]

                    def then(ins):
                        step[0] += 1
                        ins.then_inc(s_sem["dve"], 1)
                        dve.wait_ge(s_sem["dve"], STEPS * n + step[0])
                        dve.sem_inc(dve_tick, 1)

                    col = lambda i: slow_st[:, i:i + 1]
                    xx = slow_xx[:, 0:D]
                    dve.wait_ge(s_sem["x_in"], 32 * n + 32)
                    then(nc.vector.tensor_reduce(col(0), slow_x, AX.X, ALU.add))
                    then(nc.vector.tensor_scalar_mul(col(1), col(0), 1.0 / D))
                    then(nc.vector.tensor_scalar(slow_acc, slow_x, col(1), None, ALU.subtract))
                    then(nc.vector.scalar_tensor_tensor(slow_junk, slow_acc, 1.0, slow_acc, ALU.mult, ALU.mult, accum_out=col(2)))
                    then(nc.vector.tensor_scalar(col(3), col(2), 1.0 / D, EPS, ALU.mult, ALU.add))
                    then(nc.vector.tensor_scalar(col(5).bitcast(I32), col(3).bitcast(I32), 1, None, ALU.arith_shift_right))
                    then(nc.vector.tensor_copy(col(6), col(5).bitcast(I32)))
                    then(nc.vector.tensor_scalar(col(6), col(6), -1.0, float(0x5F3759DF), ALU.mult, ALU.add))
                    then(nc.vector.tensor_copy(col(5).bitcast(I32), col(6)))
                    for _ in range(4):
                        then(nc.vector.tensor_tensor(col(6), col(5), col(5), ALU.mult))
                        then(nc.vector.tensor_tensor(col(6), col(6), col(3), ALU.mult))
                        then(nc.vector.tensor_scalar(col(6), col(6), -0.5, 1.5, ALU.mult, ALU.add))
                        then(nc.vector.tensor_tensor(col(5), col(5), col(6), ALU.mult))
                    then(nc.vector.tensor_scalar(xx, slow_acc, col(5), None, ALU.mult))
                    then(nc.vector.tensor_copy(slow_xx[:, D:2 * D], xx))
                    with dve.Fori(0, D) as d:
                        nc.vector.tensor_tensor(slow_junk, xx, slow_xx[:, bass.ds(d, D)], ALU.mult).then_inc(s_lag, 1)
                        dve.wait_ge(s_lag, D * 2 * n + 2 * d + 1)
                        nc.vector.tensor_reduce(slow_corr[:, bass.ds(d, 1)], slow_junk, AX.X, ALU.add).then_inc(s_lag, 1)
                        dve.wait_ge(s_lag, D * 2 * n + 2 * d + 2)
                        dve.nop()
                    then(nc.vector.max(slow_top, slow_corr))
                    then(nc.vector.tensor_scalar_mul(slow_neg, slow_top[:, 0:1], -1.0))
                    then(nc.vector.memset(slow_top[:, TOP:8], 3.0e38))
                    then(nc.vector.match_replace(slow_mask, slow_top, slow_corr, -3.0e38))
                    nc.vector.tensor_scalar(slow_mask, slow_mask, -3.0e38, None, ALU.is_equal).then_inc(s_sem["ex_in"], 1)
                    dve.wait_ge(s_sem["act"], n + 1)
                    dve.wait_ge(s_sem["ex_in"], n + 1)
                    then(nc.vector.scalar_tensor_tensor(slow_w, slow_w, 1.0, slow_mask, ALU.mult, ALU.mult, accum_out=col(7)))
                    then(nc.vector.reciprocal(col(8), col(7)))
                    then(nc.vector.tensor_scalar(slow_w, slow_w, col(8), None, ALU.mult))
                    then(nc.vector.tensor_scalar(slow_acc, xx, -1.0, None, ALU.mult))
                    with dve.Fori(0, D) as d:
                        nc.vector.tensor_scalar(slow_junk, slow_xx[:, bass.ds(d, D)], slow_w[:, bass.ds(d, 1)], None, ALU.mult).then_inc(s_add, 1)
                        dve.wait_ge(s_add, D * 2 * n + 2 * d + 1)
                        nc.vector.tensor_tensor(slow_acc, slow_acc, slow_junk, ALU.add).then_inc(s_add, 1)
                        dve.wait_ge(s_add, D * 2 * n + 2 * d + 2)
                        dve.nop()
                    nc.vector.tensor_tensor(slow_out, slow_out, slow_acc, ALU.add).then_inc(s_sem["ob"], 1)
                    dve.nop()
            dve.nop()

        @block.gpsimd
        def _(pool):
            nc.gpsimd.memset(ident[:, :], 0.0).then_inc(pchain, 1)
            nc.gpsimd.memset(ident16[:, :], 0.0).then_inc(pchain, 1)
            nc.gpsimd.memset(ones[:, :], 1.0).then_inc(const_done, 1)
            pool.wait_ge(pchain, 2)
            for m in (ident, ident16):
                nc.gpsimd.affine_select(out=m[:, :], in_=m[:, :], compare_op=ALU.not_equal, fill=1.0, base=0,
                                        pattern=[[-1, P]], channel_multiplier=1).then_inc(const_done, 1)

            def guess(n):
                pool.wait_ge(v_done, 5 * n + 1)
                nc.gpsimd.tensor_tensor(r0[:, :], vr[:, :], mh[:, :], ALU.pow).then_inc(guess_done, 1)

            def normalise(n):
                pool.wait_ge(v_done, 5 * n + 5)
                pool.sem_inc(pool_tick, 1)
                for t in range(NT):
                    nc.gpsimd.tensor_scalar(xr[:, t, :], xr[:, t, :], nm[:, t:t + 1], rs[:, t:t + 1], ALU.add, ALU.mult).then_inc(ln_done, 1)

            def split_pair(base, q):
                pool.wait_ge(tr_sumhi, base + q + 1)
                nc.gpsimd.tensor_tensor(xop[:, q, 2, 1, :], ss[:, q % 2, :], xop[:, q, 2, 0, :], ALU.subtract).then_inc(x_ready, 1)

            guess(0)
            pool.sem_inc(pool_tick, 1)
            for q in range(QN):
                split_pair(0, q)
            nc.gpsimd.memset(pz[:, :], 0.0).then_inc(h_ready, 1)

            def gate_up(g, u):
                c, k = divmod(u, QN)
                pool.wait_ge(h_done, NU * g + u + 1)
                nc.gpsimd.tensor_tensor(hh[:, 2, :], hh[:, 0, :], hh[:, 1, :], ALU.add).then_inc(h_sum, 1)
                pool.wait_ge(h_hi, NU * g + u + 1)
                nc.gpsimd.tensor_tensor(hop[0:CH, c, k, :, 1, :], hh[:, :, :], hop[0:CH, c, k, :, 0, :], ALU.subtract).then_inc(h_ready, 1)

            def down(g, more):
                def residual(k):
                    if k:
                        pool.wait_ge(z_done, QN * g + k)
                    pool.wait_ge(zx_in[k % 2], 32 * (QN // 2 * g + k // 2 + 1))
                    pool.sem_inc(pool_tick, 1)
                    for t in range(NT):
                        last = nc.gpsimd.tensor_scalar(zt[:, :, t, :], zx[:, k % 2, :, t, :], nmd[:, t:t + 1], rsd[:, t:t + 1], ALU.add, ALU.mult)
                    last.then_inc(z_part, 1)
                    pool.wait_ge(z_part, QN * g + k + 1)
                    flat = zx[:, k % 2, :, :, :].rearrange("p b t c -> p (b t c)")
                    nc.gpsimd.tensor_tensor(flat, flat, zt[:, :, :, :].rearrange("p b t c -> p (b t c)"), ALU.add).then_inc(z_done, 1)

                def split(q):
                    split_pair(QN * g + QN, q)

                if more:
                    steps = [(residual, 0), (split, 0), (residual, 1), (split, 1), (split, 2), (residual, 2), (split, 3), (residual, 3)]
                else:
                    steps = [(residual, k) for k in range(QN)]
                for step, n in steps:
                    step(n)

            def group(g, more):
                for u in range(QN, NU):
                    gate_up(g, u)
                if more:
                    guess(g + 1)
                    normalise(g + 1)
                down(g, more)
                if more:
                    for u in range(QN):
                        gate_up(g + 1, u)

            for u in range(QN):
                gate_up(0, u)
            with pool.Fori(0, G - 1) as g:
                group(g, True)
            group(G - 1, False)


def kernel(L0_attn_x, L0_ffn_w_gate, L0_ffn_w_up, L0_ffn_w_down):
    import numpy as _np
    import concourse.bacc as _bacc
    from concourse import mybir as _mybir
    from concourse.bass_utils import run_bass_kernel_spmd as _run

    L, P = 1024, 128
    f = _np.arange(1, 257)[None, :]
    t = _np.arange(512)[:, None]
    angle = 2.0 * _np.pi * ((t * f) % 512) / 512.0
    dft = _np.concatenate([_np.cos(angle), _np.sin(angle)], axis=1).astype(_np.float16)
    dft = _np.ascontiguousarray(dft.reshape(4, P, 512).transpose(1, 0, 2))
    weight = _np.where(f == 256, 1.0, 2.0).reshape(256, 1)
    d = _np.arange(1, 257)[None, :]
    lag = weight * (1.0 - _np.cos(2.0 * _np.pi * ((f.reshape(256, 1) * d) % 512) / 512.0))
    lag = _np.concatenate([lag, 2.0 * weight, 0.0 * weight], axis=1)
    lag = _np.concatenate([lag, lag], axis=0).astype(_np.float16)
    lag = _np.ascontiguousarray(lag.reshape(4, P, 258).transpose(1, 0, 2))

    arrays = {
        "in_x": _np.ascontiguousarray(_np.asarray(L0_attn_x)[0]),
        "in_w_gate": _np.ascontiguousarray(L0_ffn_w_gate),
        "in_w_up": _np.ascontiguousarray(L0_ffn_w_up),
        "in_w_down": _np.ascontiguousarray(L0_ffn_w_down),
        "in_dft": dft,
        "in_lag": lag,
    }
    nc = _bacc.Bacc("TRN2", target_bir_lowering=False, num_devices=1)
    args = [nc.dram_tensor(n, a.shape, _mybir.dt.from_np(a.dtype), kind="ExternalInput").ap() for n, a in arrays.items()]
    out = nc.dram_tensor("out_y", (2048, L), _mybir.dt.float32, kind="ExternalOutput").ap()
    octonion_ffn_attention_kernel(nc, *args, out)
    r = _run(nc, [arrays], core_ids=[0])
    return r.results[0]["out_y"].reshape(1, 2048, L)
```

```python
def octonion_ffn_attention_kernel(nc, x, w_gate, w_up, w_down, dft, lag, out):
    import concourse.bass as bass
    from concourse import mybir
    from contextlib import ExitStack

    F32, F16, I32 = mybir.dt.float32, mybir.dt.float16, mybir.dt.int32
    ALU, ACT, AX = mybir.AluOpType, mybir.ActivationFunctionType, mybir.AxisListType

    P = 128
    ROWS, D = x.shape
    NJ, HB, DB = w_gate.shape
    QN = NJ // 2
    NC = 3
    CH = -(-HB // NC)
    HW = NC * CH
    HP = (NC - 1) * CH + P
    T = 512
    NT = T // P
    G = ROWS // T
    NU = NC * QN
    N_W = NJ * HB * DB
    EPS = 1e-5
    XS = 1024.0
    HS = 2.0 ** -6
    MARGIN = 112.0
    LAG_SCALE = 16.0
    NL = lag.shape[2]
    NQ = dft.shape[1]
    TOP = 6
    STEPS = 35
    DELTA = (1, -1, -1, 1)
    DOWN_PLACE = (14, 17, 12, 3, 9, 1, 8, 13, 18, 2, 4, 23, 0, 21, 20, 5, 7, 19, 15, 6, 22, 10, 16, 11)

    sign = [[0] * NJ for _ in range(NJ)]
    for i in range(NJ):
        sign[0][i] = sign[i][0] = 1
        if i:
            sign[i][i] = -1
    for a, b, c in [(1, 2, 3), (1, 4, 5), (1, 7, 6), (2, 4, 6), (2, 5, 7), (3, 4, 7), (3, 6, 5)]:
        for u, v in ((a, b), (b, c), (c, a)):
            sign[u][v], sign[v][u] = 1, -1
    products = []
    for k in range(QN):
        of_k = []
        for q in range(QN):
            p = k ^ q
            a, b, c, d = sign[p][q], sign[p + 4][q + 4], sign[p + 4][q], sign[p][q + 4]
            if a * d == DELTA[k]:
                of_k.append([(0, 2, (p, a, 0)), (1, 1, (p, -a, b)), (2, 0, (p, -d, c))])
            else:
                of_k.append([(0, 2, (p, 0, b)), (1, 0, (p, a, -b)), (2, 1, (p, d, -c))])
        products.append(of_k)
    slots = sorted({w for of_k in products for of_q in of_k for _, _, w in of_q})
    slot_of = {w: n for n, w in enumerate(slots)}
    NS = len(slots)

    down_place = dict(zip(slots, DOWN_PLACE))

    def run(items):
        steps = {(b[0] - a[0], b[1] - a[1]) for a, b in zip(items, items[1:])}
        (dk, ds), = steps if len(steps) == 1 else ((1, 1),) if not steps else ((0, 0),)
        return (items[0][0], dk, len(items), items[0][1], ds) if dk > 0 and ds > 0 else None

    def fewest(items):
        if run(items):
            return [run(items)]
        if len(items) == 2:
            return fewest(items[:1]) + fewest(items[1:])
        cuts = [((items[0], items[i]), tuple(x for x in items[1:] if x is not items[i])) for i in range(1, len(items))]
        return min((fewest(a) + fewest(b) for a, b in cuts), key=len)

    down_runs = [[[] for _ in range(3)] for _ in range(QN)]
    for q in range(QN):
        for o in range(3):
            for a in range(3):
                items = tuple((k, down_place[w]) for k in range(QN) for a_k, o_k, w in products[k][q] if (a_k, o_k) == (a, o))
                if items:
                    down_runs[q][o] += [(a,) + r for r in fewest(items)]

    ctx = ExitStack()
    with ctx:
        def sb(name, shape, dt):
            return ctx.enter_context(nc.sbuf_tensor(name, shape, dt))

        def sem(name):
            return ctx.enter_context(nc.semaphore(name))

        wg = sb("wg", [P, NS, HP], F16)
        wu = sb("wu", [P, NS, HP], F16)
        wd = sb("wd", [CH, NS, NC, DB], F16)
        xop = sb("xop", [P, QN, 3, 2, T], F16)
        hop = sb("hop", [P, NC, QN, 3, 2, T], F16)
        xr = sb("xr", [P, NT, D], F32)
        zx = sb("zx", [P, 2, D], F32)
        zt = sb("zt", [P, D], F32)
        kb = sb("kb", [P, T], F32)
        gb = sb("gb", [CH, 2, T], F32)
        hh = sb("hh", [CH, 3, T], F32)
        yt = sb("yt", [P, 2, T], F32)
        pw = yt[:, 0, :].bitcast(F16).rearrange("p (m t) -> p m t", t=T)
        xs = sb("xs", [P, 2, T], F32)
        ss = sb("ss", [P, 2, T], F32)
        junk = zt[:, :]
        fold = sb("fold", [P, NQ, T], F16)
        dft_sb = sb("dft_sb", [P, NQ, NQ * P], F16)
        lag_sb = sb("lag_sb", [P, NQ, NL], F16)
        ident = sb("ident", [P, P], F32)
        ident16 = sb("ident16", [P, P], F16)
        ones = sb("ones", [P, P], F32)
        asum = sb("asum", [P, 3, 2], F32)
        tot = sb("tot", [P, 3], F32)
        thr = sb("thr", [P, 3], F32)
        nthr = sb("nthr", [P, 3], F32)
        gsc = sb("gsc", [P, 1], F32)
        hsc = sb("hsc", [P, 1], F32)
        osc = sb("osc", [P, 1], F32)
        sm = sb("sm", [P, NT], F32)
        nm = sb("nm", [P, NT], F32)
        vr = sb("vr", [P, NT], F32)
        r0 = sb("r0", [P, NT], F32)
        rr = sb("rr", [P, NT], F32)
        rs = sb("rs", [P, NT], F32)
        nmd = sb("nmd", [P, NT], F32)
        rsd = sb("rsd", [P, NT], F32)
        mh = sb("mh", [P, NT], F32)
        dmin = sb("dmin", [P, NT], F32)
        rmin = sb("rmin", [P, NT], F32)
        dots = sb("dots", [P, NT], F32)
        hb = sb("hb", [P, NT], F32)
        fl = sb("fl", [P, NT], F32)
        fs = sb("fs", [P, 1], F32)
        flag = sb("flag", [P, 1], I32)
        pz = sb("pz", [P, 1], F32)

        prep = hop[:, :, :, :, :, :].rearrange("p c k o h t -> p (c k o h t)")
        stage, tern, wt = [], [], []
        for m in range(3):
            stage.append(prep[:, 6144 * m:6144 * (m + 1)].bitcast(F32))
            tern.append(prep[:, 18432 + 3072 * m:18432 + 3072 * (m + 1)])
            wt.append(prep[:, 27648 + 3072 * m:27648 + 3072 * (m + 1)])

        slow = prep.bitcast(F32)
        slow_x = slow[:, 0:D]
        slow_out = slow[:, D:2 * D]
        slow_corr = slow[:, 2 * D:3 * D]
        slow_w = slow[:, 3 * D:4 * D]
        slow_xx = slow[:, 4 * D:6 * D]
        slow_acc = slow[:, 6 * D:7 * D]
        slow_junk = slow[:, 7 * D:8 * D]
        slow_mask = slow[:, 8 * D:9 * D]
        slow_top = slow[:, 9 * D:9 * D + 8]
        slow_neg = slow[:, 9 * D + 8:9 * D + 9]
        slow_st = slow[:, 9 * D + 16:9 * D + 32]

        acc = ctx.enter_context(nc.psum_tensor("acc", [P, 2, 3, T], F32))
        side = ctx.enter_context(nc.psum_tensor("side", [P, 2, T], F32))

        first_banks = (side, acc[:, 1, 1:3, :])

        def weight_bank(n):
            if n >= NJ:
                return side[:, n % 2, :].bitcast(F16)
            return acc[:, n % 4 // 3, n % 4 % 3, :].bitcast(F16)

        def total_bank(m):
            return side[:, m % 2, 0:2]

        x_in = [sem(f"x_in{t}") for t in range(NT)]; w_in = [sem(f"w_in{m}") for m in range(3)]; tab_in = sem("tab_in"); zx_in = [sem(f"zx_in{n}") for n in range(2)]
        const_done = sem("const_done"); abs_done = [sem(f"abs_done{m}") for m in range(3)]; total_done = [sem(f"total_done{m}") for m in range(3)]
        total_read = sem("total_read"); thr_done = sem("thr_done"); neg_done = sem("neg_done"); tern_done = sem("tern_done"); wt_mm = sem("wt_mm"); wt_copied = sem("wt_copied")
        down_ready = sem("down_ready"); slots_ready = sem("slots_ready")
        sum_done = sem("sum_done"); mean_done = sem("mean_done"); var_done = sem("var_done"); v_done = sem("v_done")
        guess_done = sem("guess_done"); ln_done = sem("ln_done")
        tr_mm = sem("tr_mm"); tr_hi = sem("tr_hi"); xs_done = sem("xs_done"); ss_done = sem("ss_done"); tr_sum = sem("tr_sum"); tr_sumhi = sem("tr_sumhi"); x_ready = sem("x_ready")
        gate_mm = sem("gate_mm"); up_mm = sem("up_mm"); down_mm = sem("down_mm"); k_copied = sem("k_copied")
        acc0_read = sem("acc0_read"); acc1_read = sem("acc1_read"); silu_done = sem("silu_done"); h_done = sem("h_done")
        h_sum = sem("h_sum"); h_hi = sem("h_hi"); h_ready = sem("h_ready")
        dot_done = sem("dot_done"); fold_part = sem("fold_part"); fold_done = sem("fold_done")
        dft_mm = sem("dft_mm"); power_done = sem("power_done"); lag_mm = sem("lag_mm"); bound_done = sem("bound_done")
        z_done = sem("z_done"); out_done = sem("out_done"); out_st = sem("out_st")
        chain = sem("chain"); pchain = sem("pchain"); flag_sum = sem("flag_sum"); flag_mm = sem("flag_mm"); flag_done = sem("flag_done")
        s_sem = {n: sem("slow_" + n) for n in ("x_in", "ex_in", "dve", "act", "st", "ob")}
        pool_tick = sem("pool_tick"); dve_tick = sem("dve_tick")
        kept = sem("kept")
        zeroed = sem("zeroed")
        least_done = sem("least_done")
        z_part = sem("z_part")
        s_lag = sem("slow_lag"); s_add = sem("slow_add")
        acc_read = (acc0_read, acc1_read)
        PER = NU + 2

        x_rows = x.rearrange("(n p) d -> n p d", p=P)
        block = ctx.enter_context(nc.Block())

        last_rows = HB - (NC - 1) * CH
        three = lambda a, w: a.rearrange("p (j d) -> p j d", j=NJ)[:, :, 0:w]
        parts = []
        for m in range(2):
            full, rest = slice(0, 2 * NJ * DB), slice(2 * NJ * DB, 3 * NJ * DB)
            parts.append([(stage[m][0:CH, full], tern[m][0:CH, full], wt[m][0:CH, full]),
                          (stage[m][0:last_rows, rest], tern[m][0:last_rows, rest], wt[m][0:last_rows, rest])])
        parts.append([(stage[2][:, 0:NJ * HB], three(tern[2][:, 0:NJ * HW], HB), wt[2][:, 0:NJ * HB])])

        @block.sync
        def _(sp):
            sp.wait_ge(w_in[1], 48)
            for t in range(NT):
                sp.dma_start(xr[:, t, :], x_rows[t, :, :]).then_inc(x_in[t], 16)
            sp.dma_start(stage[2][:, 0:NJ * HB].rearrange("p (j d) -> p j d", j=NJ), w_down.rearrange("j o d -> o j d")).then_inc(w_in[2], 16)
            for t in range(2):
                sp.dma_start(zx[:, t, :], x_rows[t, :, :]).then_inc(zx_in[t], 16)
            sp.dma_start(dft_sb[:, :, :], dft).then_inc(tab_in, 16)
            sp.dma_start(lag_sb[:, :, :], lag).then_inc(tab_in, 16)

            def group(g, more):
                if more:
                    sp.wait_ge(dot_done, NT * g + NT)
                    sp.wait_ge(tr_mm, QN * g + QN)
                    for t in range(NT):
                        sp.dma_start(xr[:, t, :], x[bass.ds(T * g + T + P * t, P), :]).then_inc(x_in[t], 16)
                for t in range(NT):
                    sp.wait_ge(out_done, NT * g + t + 1)
                    sp.dma_start(out[bass.ds(T * g + P * t, P), :], zx[:, t % 2, :]).then_inc(out_st, 16)
                    if t + 2 < NT or more:
                        sp.wait_ge(out_st, 16 * (NT * g + t + 1))
                        sp.dma_start(zx[:, t % 2, :], x[bass.ds(T * g + P * (t + 2), P), :]).then_inc(zx_in[t % 2], 16)

            with sp.Fori(0, G - 1) as g:
                group(g, True)
            group(G - 1, False)
            sp.wait_ge(out_st, 16 * NT * G)
            sp.nop()

        @block.tensor
        def _(pe):
            pe.wait_ge(const_done, 3)

            def total(m):
                pe.wait_ge(abs_done[m], 2 if m < 2 else 1)
                nc.tensor.matmul(total_bank(m), ones[:, :], asum[:, m, :], start=True, stop=True).then_inc(total_done[m], 1)

            def transpose_weights(m, bankfuls=range(NJ // 2)):
                pe.wait_ge(tern_done, m + 1)
                for jj in bankfuls:
                    n = NJ // 2 * m + jj
                    if 4 <= n < NJ or n >= NJ + 2:
                        pe.wait_ge(wt_copied, n - 3 if n < NJ else n - 1)
                    bank = weight_bank(n)
                    for j in range(2):
                        for c in range(NC):
                            if m < 2:
                                src = tern[m][0:CH, :].rearrange("p (c j d) -> p c j d", c=NC, j=NJ)[:, c, 2 * jj + j, :]
                                dst = bank[:, HW * j + CH * c:HW * j + CH * (c + 1)]
                                last = nc.tensor.transpose(dst, src, ident16[0:CH, 0:CH])
                            else:
                                src = tern[m][:, 0:NJ * HW].rearrange("p (j d) -> p j d", j=NJ)[:, 2 * jj + j, CH * c:CH * (c + 1)]
                                dst = bank[0:CH, (NC * j + c) * DB:(NC * j + c + 1) * DB]
                                last = nc.tensor.transpose(dst, src, ident16[:, :])
                    last.then_inc(wt_mm, 1)

            def transpose_pair(q, banks):
                for b in range(2):
                    for t in range(NT):
                        i = QN * b + q
                        last = nc.tensor.transpose(banks[:, b, t * P:(t + 1) * P], xr[:, t, i * DB:(i + 1) * DB], ident[:, :])
                last.then_inc(tr_mm, 1)

            total(0)
            transpose_weights(0)
            total(1)
            transpose_weights(1)
            pe.wait_ge(ln_done, NT)
            for q in range(QN):
                if q == 0:
                    pe.wait_ge(total_read, 2)
                if q >= 2:
                    pe.wait_ge(tr_sum, q - 1)
                transpose_pair(q, first_banks[q % 2])
            pe.wait_ge(wt_copied, NJ)

            def triple(half, w, operands, k, first, last_chunk, before=lambda q: None):
                for q in range(QN):
                    before(q)
                    for a, o, slot in products[k][q]:
                        for h in range(2):
                            last = nc.tensor.matmul(acc[:, half, a, :], w(slot_of[slot]), operands(q, o, h),
                                                    start=first and q == 0 and h == 0,
                                                    stop=last_chunk and q == QN - 1 and h == 1)
                return last

            def gate_up(g, u):
                c, k = divmod(u, QN)

                def before(q):
                    if u == 0:
                        pe.wait_ge(tr_sum, QN * g + q + 1)
                        pe.wait_ge(x_ready, QN * g + q + 1)

                for half, w, done in ((0, wg, gate_mm), (1, wu, up_mm)):
                    pe.wait_ge(acc_read[half], PER * g + u + 1)
                    if u == QN:
                        pe.wait_ge(slots_ready, half + 1)
                    triple(half, lambda s, w=w: w[:, s, CH * c:CH * c + P], lambda q, o, h: xop[:, q, o, h, :],
                           k, True, True, before if half == 0 else lambda q: None).then_inc(done, 1)
                if 3 <= u < 3 + NQ:
                    m = u - 3
                    if m == 0:
                        pe.wait_ge(tab_in, 32)
                        pe.wait_ge(wt_copied, 12)
                        pe.wait_ge(tr_sum, QN * g + QN)
                        pe.wait_ge(fold_done, g + 1)
                    for q in range(NQ):
                        last = nc.tensor.matmul(side[:, m, :], dft_sb[:, q, m * P:(m + 1) * P], fold[:, q, :],
                                                start=q == 0, stop=q == NQ - 1)
                    last.then_inc(dft_mm, 1)
                if 7 <= u < 11:
                    t = u - 7
                    if t < 2:
                        pe.wait_ge(power_done, NQ * g + NQ)
                    else:
                        pe.wait_ge(bound_done, NT * g + t - 1)
                    for m in range(NQ):
                        last = nc.tensor.matmul(side[:, t % 2, 0:NL], pw[:, m, t * P:(t + 1) * P], lag_sb[:, m, :],
                                                start=m == 0, stop=m == NQ - 1)
                    last.then_inc(lag_mm, 1)

            def down(g, more):
                def next_pair(q):
                    if q == 0:
                        pe.wait_ge(ln_done, NT * g + 2 * NT)
                        pe.wait_ge(bound_done, NT * g + NT)
                    else:
                        pe.wait_ge(tr_sum, QN * g + QN + q)
                    transpose_pair(q, side)

                between = {(1, 0): 0, (1, 2): 1, (2, 1): 2, (3, 0): 3} if more else {}
                for t in range(NT):
                    half = t % 2
                    pe.wait_ge(acc_read[half], PER * g + NU + t // 2 + 1)
                    order = [(c, q, o, h, piece) for c in range(NC) for q in range(QN) for o in range(3) for h in range(2)
                             for piece in down_runs[q][o]]
                    firsts = {next(i for i, x in enumerate(order) if x[4][0] == a) for a in range(3)}
                    lasts = {max(i for i, x in enumerate(order) if x[4][0] == a) for a in range(3)}
                    n = 0
                    for c in range(NC):
                        if t == 0:
                            pe.wait_ge(h_ready, NU * g + QN * (c + 1) + 1)
                            if c == 0:
                                pe.wait_ge(down_ready, 1)
                        for q in range(QN):
                            for o in range(3):
                                for h in range(2):
                                    for a, k0, dk, count, s0, ds in down_runs[q][o]:
                                        columns = acc[:, half, a, :].rearrange("p (k c) -> p k c", c=DB)[:, k0:k0 + dk * (count - 1) + 1:dk, :]
                                        last = nc.tensor.matmul(columns, hop[0:CH, c, q, o, h, P * t:P * (t + 1)],
                                                                wd[:, s0:s0 + ds * (count - 1) + 1:ds, c, :],
                                                                start=n in firsts, stop=n in lasts)
                                        n += 1
                        if c == NC - 1:
                            last.then_inc(down_mm, 1)
                        if (t, c) in between:
                            next_pair(between[t, c])
                        if (t, c) == (1, 0) and not more:
                            pe.wait_ge(flag_sum, 1)
                            nc.tensor.matmul(side[:, 0, 0:1], ones[:, :], fs[:, :], start=True, stop=True).then_inc(flag_mm, 1)

            def group(g, more):
                for u in range(QN, NU):
                    gate_up(g, u)
                down(g, more)
                if more:
                    for u in range(QN):
                        gate_up(g + 1, u)

            gate_up(0, 0)
            total(2)
            gate_up(0, 1)
            pe.wait_ge(total_read, 3)
            transpose_weights(2, (0, 1))
            gate_up(0, 2)
            transpose_weights(2, (2, 3))
            gate_up(0, 3)
            with pe.Fori(0, G - 1) as g:
                group(g, True)
            group(G - 1, False)

        @block.scalar
        def _(act):
            for m, w in ((0, w_gate), (1, w_up)):
                dst = stage[m].rearrange("p (c j d) -> p c j d", c=NC, j=NJ)
                for c in range(NC):
                    n = min(CH, HB - CH * c)
                    act.dma_start(dst[0:n, c, :, :], w[:, CH * c:CH * c + n, :].rearrange("j o d -> o j d")).then_inc(w_in[m], 16)

            def row_sum(n, t, first=False):
                act.wait_ge(x_in[t], 16 * (n + 1))
                if t:
                    act.wait_ge(sum_done, NT * n + t)
                elif not first:
                    act.wait_ge(var_done, NT * n)
                nc.scalar.activation(junk, xr[:, t, :], ACT.Copy, accum_out=sm[:, t:t + 1]).then_inc(sum_done, 1)

            def row_var(n, t):
                act.wait_ge(mean_done, n + 1)
                if t:
                    act.wait_ge(var_done, NT * n + t)
                else:
                    act.wait_ge(sum_done, NT * n + NT)
                nc.scalar.activation(junk, xr[:, t, :], ACT.Square, bias=nm[:, t:t + 1], accum_out=vr[:, t:t + 1]).then_inc(var_done, 1)

            def pair_heads(base, q, banks):
                act.wait_ge(tr_mm, base + q + 1)
                if q >= 2:
                    act.wait_ge(ss_done, base + q - 1)
                nc.scalar.activation(xop[:, q, 1, 0, :], banks[:, 1, :], ACT.Copy, scale=XS)
                nc.scalar.activation(xs[:, q % 2, :], banks[:, 0, :], ACT.Copy, scale=XS).then_inc(xs_done, 1)
                nc.scalar.activation(xop[:, q, 0, 0, :], banks[:, 0, :], ACT.Copy, scale=XS).then_inc(tr_hi, 1)

            def sum_head(base, q):
                act.wait_ge(ss_done, base + q + 1)
                nc.scalar.activation(xop[:, q, 2, 0, :], ss[:, q % 2, :], ACT.Copy).then_inc(tr_sumhi, 1)

            def absolute(m, n):
                act.wait_ge(w_in[m], 16 * (3 if m < 2 else 1))
                src, val, _ = parts[m][n]
                if m == 2:
                    src = three(src, HB)
                nc.scalar.activation(val, src, ACT.Abs, accum_out=asum[0:src.shape[0], m, n:n + 1]).then_inc(abs_done[m], 1)

            def weights_out(m, bankfuls=range(NJ // 2)):
                for jj in bankfuls:
                    n = NJ // 2 * m + jj
                    act.wait_ge(wt_mm, n + 1)
                    rows, width = (P, HW) if m < 2 else (CH, NC * DB)
                    nc.scalar.activation(wt[m][0:rows, 2 * width * jj:2 * width * (jj + 1)], weight_bank(n)[0:rows, 0:2 * width], ACT.Copy).then_inc(wt_copied, 1)

            act.wait_ge(zeroed, 1)
            absolute(0, 1)
            absolute(1, 0)
            for t in range(NT):
                row_sum(0, t, first=True)
            for t in range(NT):
                row_var(0, t)
            absolute(2, 0)
            weights_out(1)
            pair_heads(0, 0, first_banks[0])
            pair_heads(0, 1, first_banks[1])
            for q in range(2, QN):
                sum_head(0, q - 2)
                pair_heads(0, q, first_banks[q % 2])
            sum_head(0, QN - 2)
            sum_head(0, QN - 1)

            def gate_up(g, u, more):
                c, k = divmod(u, QN)
                act.wait_ge(gate_mm, NU * g + u + 1)
                act.wait_ge(acc1_read, PER * g + u + 1)
                nc.scalar.activation(kb[0:CH, :], acc[0:CH, 0, 0, :], ACT.Copy).then_inc(k_copied, 1)
                act.wait_ge(acc0_read, PER * g + u + 2)
                nc.scalar.activation(gb[:, :, :], gb[:, :, :], ACT.Silu, scale=gsc[0:CH, :]).then_inc(silu_done, 1)
                act.wait_ge(up_mm, NU * g + u + 1)
                nc.scalar.activation(kb[0:CH, :], acc[0:CH, 1, 0, :], ACT.Copy).then_inc(k_copied, 1)
                if 3 <= u < 3 + NQ:
                    m = u - 3
                    act.wait_ge(dft_mm, NQ * g + m + 1)
                    nc.scalar.activation(pw[:, m, :], side[:, m, :], ACT.Square, scale=1.0 / (4.0 * XS)).then_inc(power_done, 1)
                if more and 4 <= u < 8:
                    row_sum(g + 1, u - 4)
                if more and 8 <= u < 12:
                    row_var(g + 1, u - 8)
                act.wait_ge(h_sum, NU * g + u + 1)
                nc.scalar.activation(hop[0:CH, c, k, :, 0, :], hh[:, :, :], ACT.Copy).then_inc(h_hi, 1)

            def down(g, more):
                def k_out(t):
                    act.wait_ge(down_mm, NT * g + t + 1)
                    act.wait_ge(acc_read[(t + 1) % 2], PER * g + NU + (t + 1) // 2 + 1)
                    nc.scalar.activation(kb[:, :], acc[:, t % 2, 0, :], ACT.Copy).then_inc(k_copied, 1)

                def split(q):
                    pair_heads(QN * g + QN, q, side)
                    sum_head(QN * g + QN, q)

                if more:
                    steps = [(k_out, 0), (split, 0), (split, 1), (k_out, 1), (split, 2), (k_out, 2), (split, 3), (k_out, 3)]
                else:
                    steps = [(k_out, t) for t in range(NT)]
                for step, n in steps:
                    step(n)

            def group(g, more):
                for u in range(QN, NU):
                    gate_up(g, u, more)
                down(g, more)
                if more:
                    for u in range(QN):
                        gate_up(g + 1, u, True)

            gate_up(0, 0, True)
            gate_up(0, 1, True)
            weights_out(2, (0, 1))
            gate_up(0, 2, True)
            weights_out(2, (2, 3))
            gate_up(0, 3, True)
            with act.Fori(0, G - 1) as g:
                group(g, True)
            group(G - 1, False)

            act.wait_ge(flag_done, 1)
            rows_left = act.value_load(flag[0:1, 0:1])
            with act.If(rows_left > 0):
                act.wait_ge(out_st, 16 * NT * G)
                with act.Fori(0, ROWS // P) as n:
                    act.dma_start(slow_x[:, :], x[bass.ds(P * n, P), :]).then_inc(s_sem["x_in"], 16)
                    act.dma_start(slow_out[:, :], out[bass.ds(P * n, P), :]).then_inc(s_sem["x_in"], 16)
                    act.wait_ge(s_sem["ex_in"], n + 1)
                    nc.scalar.activation(slow_w[:, :], slow_corr[:, :], ACT.Exp, bias=slow_neg[:, :]).then_inc(s_sem["act"], 1)
                    act.wait_ge(s_sem["ob"], n + 1)
                    act.dma_start(out[bass.ds(P * n, P), :], slow_out[:, :]).then_inc(s_sem["st"], 16)
                    act.wait_ge(s_sem["st"], 16 * n + 16)
                    act.nop()
            act.nop()

        @block.vector
        def _(dve):
            count = [0]

            def link(ins):
                count[0] += 1
                ins.then_inc(chain, 1)
                dve.wait_ge(chain, count[0])

            nc.vector.memset(rmin[:, :], 3.0e38)
            for w in (wg, wu):
                nc.vector.memset(w[:, :, HW:HP], 0.0)
            nc.vector.memset(mh[:, :], -0.5)
            for m in range(2):
                nc.vector.memset(tern[m][0:CH, 2 * NJ * DB:3 * NJ * DB], 0.0)
            nc.vector.memset(tern[2][:, 0:NJ * HW].rearrange("p (j d) -> p j d", j=NJ)[:, :, HB:HW], 0.0)
            nc.vector.memset(asum[:, :, :], 0.0).then_inc(zeroed, 1)
            dve.wait_ge(zeroed, 1)

            def keep_stats(g):
                nc.vector.tensor_copy(nmd[:, :], nm[:, :])
                nc.vector.tensor_copy(rsd[:, :], rs[:, :]).then_inc(kept, 1)
                dve.wait_ge(kept, g + 1)

            def mean(n):
                dve.wait_ge(sum_done, NT * n + NT)
                nc.vector.tensor_scalar_mul(nm[:, :], sm[:, :], -1.0 / D).then_inc(mean_done, 1)

            def tiny(ins, at):
                ins.then_inc(v_done, 1)
                dve.wait_ge(v_done, at)

            def variance(n):
                dve.wait_ge(var_done, NT * n + NT)
                nc.vector.tensor_scalar(vr[:, :], vr[:, :], 1.0 / D, EPS, ALU.mult, ALU.add).then_inc(v_done, 1)

            def rstd(n):
                dve.wait_ge(guess_done, n + 1)
                tiny(nc.vector.tensor_tensor(rr[:, :], r0[:, :], r0[:, :], ALU.mult), 5 * n + 2)
                tiny(nc.vector.tensor_tensor(rr[:, :], rr[:, :], vr[:, :], ALU.mult), 5 * n + 3)
                tiny(nc.vector.tensor_scalar(rr[:, :], rr[:, :], -0.5, 1.5, ALU.mult, ALU.add), 5 * n + 4)
                tiny(nc.vector.tensor_tensor(rs[:, :], r0[:, :], rr[:, :], ALU.mult), 5 * n + 5)

            def thresholds(m):
                dve.wait_ge(total_done[m], 1)
                nc.vector.tensor_reduce(tot[:, m:m + 1], total_bank(m), AX.X, ALU.add).then_inc(total_read, 1)
                dve.wait_ge(total_read, m + 1)
                link(nc.vector.tensor_scalar_mul(thr[:, m:m + 1], tot[:, m:m + 1], 0.5 / N_W))
                nc.vector.tensor_scalar_mul(nthr[:, m:m + 1], tot[:, m:m + 1], -0.5 / N_W).then_inc(thr_done, 1)
                dve.wait_ge(thr_done, m + 1)

            def ternary(m, between=None):
                src, _, neg = parts[m][0]
                link(nc.vector.tensor_scalar(neg, src, nthr[0:src.shape[0], m:m + 1], None, ALU.is_lt))
                if between:
                    between()
                for n, (src, val, neg) in enumerate(parts[m]):
                    if m == 2:
                        src, neg = three(src, HB), three(neg, HB)
                    if n == 1:
                        dve.wait_ge(neg_done, m + 1)
                    last = nc.vector.scalar_tensor_tensor(val, src, thr[0:src.shape[0], m:m + 1], neg, ALU.is_gt, ALU.subtract)
                last.then_inc(tern_done, 1)

            def weight_slots(m, lo, hi, ready, some=slice(0, NS)):
                dve.wait_ge(wt_copied, NJ // 2 * (m + 1))
                rows, width = (P, HW) if m < 2 else (CH, NC * DB)
                part = lambda j: wt[m][0:rows, width * j + lo:width * j + hi]
                for n, (p, ca, cb) in list(enumerate(slots))[some]:
                    dst = (wg[:, n, :], wu[:, n, :], wd[:, down_place[slots[n]], :, :].rearrange("p c d -> p (c d)"))[m][:, lo:hi]
                    if not (ca and cb):
                        last = nc.vector.tensor_scalar_mul(dst, part(p if ca else p + 4), float(ca + cb))
                    elif ca == cb == -1:
                        last = nc.vector.scalar_tensor_tensor(dst, part(p), -1.0, part(p + 4), ALU.mult, ALU.subtract)
                    elif ca == 1:
                        last = nc.vector.tensor_tensor(dst, part(p), part(p + 4), ALU.add if cb == 1 else ALU.subtract)
                    else:
                        last = nc.vector.tensor_tensor(dst, part(p + 4), part(p), ALU.subtract)
                if ready:
                    last.then_inc(ready, 1)

            def split_pair(base, q, banks):
                if q >= 2:
                    dve.wait_ge(x_ready, base + q - 1)
                dve.wait_ge(xs_done, base + q + 1)
                nc.vector.scalar_tensor_tensor(ss[:, q % 2, :], banks[:, 1, :], XS, xs[:, q % 2, :], ALU.mult, ALU.add).then_inc(ss_done, 1)
                for b in (1, 0):
                    if b == 0:
                        dve.wait_ge(tr_hi, base + q + 1)
                    last = nc.vector.scalar_tensor_tensor(xop[:, q, b, 1, :], banks[:, b, :], XS, xop[:, q, b, 0, :], ALU.mult, ALU.subtract)
                last.then_inc(tr_sum, 1)

            def absolute(m, n):
                dve.wait_ge(w_in[m], 48)
                src = parts[m][n][0]
                nc.vector.tensor_reduce(asum[0:src.shape[0], m, n:n + 1], src, AX.X, ALU.add, apply_absolute_value=True).then_inc(abs_done[m], 1)

            absolute(0, 0)
            thresholds(0)
            ternary(0)
            absolute(1, 1)
            for n in range(NJ // 2):
                dve.wait_ge(wt_mm, n + 1)
                nc.vector.tensor_copy(wt[0][:, 2 * HW * n:2 * HW * (n + 1)], weight_bank(n)[:, 0:2 * HW]).then_inc(wt_copied, 1)
            thresholds(1)
            ternary(1, lambda: mean(0))
            weight_slots(0, 0, P, None, slice(0, NS // 2))
            variance(0)
            weight_slots(0, 0, P, acc0_read, slice(NS // 2, NS))
            rstd(0)
            for t in range(NT // 2):
                nc.vector.tensor_scalar(xr[:, t, :], xr[:, t, :], nm[:, t:t + 1], rs[:, t:t + 1], ALU.add, ALU.mult).then_inc(ln_done, 1)
            for q in range(QN):
                split_pair(0, q, first_banks[q % 2])
            weight_slots(1, 0, P, acc1_read)
            link(nc.vector.tensor_scalar_mul(gsc[:, :], thr[:, 0:1], 2.0 / XS))
            link(nc.vector.reciprocal(hsc[:, :], thr[:, 0:1]))
            link(nc.vector.tensor_scalar_mul(hsc[:, :], hsc[:, :], 0.5 * HS / XS))

            def out_of_k(rows, half, k, dst):
                nc.vector.tensor_tensor(dst[:, 0, :], acc[0:rows, half, 1, :], kb[0:rows, :], ALU.add)
                return nc.vector.tensor_tensor(dst[:, 1, :], acc[0:rows, half, 2, :], kb[0:rows, :],
                                               ALU.add if DELTA[k] == 1 else ALU.subtract)

            def halves(n):
                dve.wait_ge(ln_done, NT * n + NT)
                for t in range(NT):
                    nc.vector.scalar_tensor_tensor(fold[:, 0, :], xr[:, t, 0:D // 2], 1.0, xr[:, t, D // 2:D], ALU.mult, ALU.mult,
                                                   accum_out=dots[:, t:t + 1]).then_inc(dot_done, 1)
                    dve.wait_ge(dot_done, NT * n + t + 1)

            def fold_rows(g):
                dve.wait_ge(x_ready, QN * g + QN)
                nc.vector.tensor_scalar_mul(fold[:, :, :], xop[:, NQ:2 * NQ, 2, 0, :], 0.5).then_inc(fold_part, 1)
                dve.wait_ge(fold_part, g + 1)
                nc.vector.scalar_tensor_tensor(fold[:, :, :], xop[:, 0:NQ, 2, 0, :], 0.5, fold[:, :, :], ALU.mult, ALU.subtract).then_inc(fold_done, 1)

            def least(g):
                def then(ins, n):
                    ins.then_inc(least_done, 1)
                    dve.wait_ge(least_done, 5 * g + n)
                then(nc.vector.tensor_tensor(hb[:, :], rsd[:, :], rsd[:, :], ALU.mult), 1)
                then(nc.vector.tensor_scalar(hb[:, :], hb[:, :], -LAG_SCALE * D * EPS, LAG_SCALE * D, ALU.mult, ALU.add), 2)
                dve.wait_ge(bound_done, NT * g + NT)
                then(nc.vector.scalar_tensor_tensor(hb[:, :], dots[:, :], -2.0 * LAG_SCALE, hb[:, :], ALU.mult, ALU.add), 3)
                then(nc.vector.tensor_tensor(hb[:, :], hb[:, :], dmin[:, :], ALU.min), 4)
                then(nc.vector.tensor_tensor(rmin[:, :], rmin[:, :], hb[:, :], ALU.min), 5)

            def gate_up(g, u, more, between=None):
                c, k = divmod(u, QN)
                dve.wait_ge(k_copied, (2 * NU + NT) * g + 2 * u + 1)
                out_of_k(CH, 0, k, gb).then_inc(acc0_read, 1)
                if between:
                    between()
                dve.wait_ge(k_copied, (2 * NU + NT) * g + 2 * u + 2)
                dve.wait_ge(h_ready, NU * g + u + 1)
                out_of_k(CH, 1, k, hh).then_inc(acc1_read, 1)
                dve.wait_ge(silu_done, NU * g + u + 1)
                dve.wait_ge(acc1_read, PER * g + u + 2)
                nc.vector.scalar_tensor_tensor(hh[:, 0:2, :], gb[:, :, :], hsc[0:CH, :], hh[:, 0:2, :], ALU.mult, ALU.mult).then_inc(h_done, 1)
                if u == 2:
                    fold_rows(g)
                if u == 7:
                    keep_stats(g)
                    if more:
                        mean(g + 1)
                if 7 <= u < 11:
                    t = u - 7
                    dve.wait_ge(lag_mm, NT * g + t + 1)
                    nc.vector.tensor_reduce(dmin[:, t:t + 1], side[:, t % 2, 0:NL], AX.X, ALU.min).then_inc(bound_done, 1)
                if u == 11:
                    if more:
                        variance(g + 1)
                    least(g)
                    if more:
                        rstd(g + 1)

            def down(g, more):
                def down_y(t):
                    if t == 0:
                        dve.wait_ge(lag_mm, NT * g + NT)
                    else:
                        dve.wait_ge(out_done, NT * g + t)
                    dve.wait_ge(k_copied, (2 * NU + NT) * g + 2 * NU + t + 1)
                    nc.vector.tensor_tensor(yt[:, 0, :], acc[:, t % 2, 1, :], kb[:, :], ALU.add)
                    by_part = lambda a: a.rearrange("p (k c) -> p k c", c=DB)
                    for delta, ks in ((-1, slice(1, 3)), (1, slice(0, QN, 3))):
                        last = nc.vector.tensor_tensor(by_part(yt[:, 1, :])[:, ks, :], by_part(acc[:, t % 2, 2, :])[:, ks, :],
                                                       by_part(kb[:, :])[:, ks, :], ALU.add if delta == 1 else ALU.subtract)
                    last.then_inc(acc_read[t % 2], 1)

                def finish(t):
                    dve.wait_ge(z_done, NT * g + t + 1)
                    dve.wait_ge(acc_read[t % 2], PER * g + NU + t // 2 + 2)
                    nc.vector.scalar_tensor_tensor(zx[:, t % 2, :], yt[:, :, :].rearrange("p b c -> p (b c)"), osc[:, :],
                                                   zx[:, t % 2, :], ALU.mult, ALU.add).then_inc(out_done, 1)

                def split(q):
                    split_pair(QN * g + QN, q, side)

                def count_rows(_):
                    link(nc.vector.tensor_scalar(fl[:, :], rmin[:, :], MARGIN * LAG_SCALE, None, ALU.is_lt))
                    nc.vector.tensor_reduce(fs[:, :], fl[:, :], AX.X, ALU.add).then_inc(flag_sum, 1)

                def flag_out(_):
                    dve.wait_ge(flag_mm, 1)
                    nc.vector.tensor_copy(flag[:, :], side[:, 0, 0:1]).then_inc(flag_done, 1)

                if more:
                    steps = [(down_y, 0), (finish, 0), (split, 0), (halves, g + 1), (split, 1), (down_y, 1), (finish, 1), (split, 2),
                             (down_y, 2), (finish, 2), (split, 3), (down_y, 3), (finish, 3)]
                else:
                    steps = [(count_rows, 0)] + [(step, t) for t in range(NT - 1) for step in (down_y, finish)]
                    steps += [(flag_out, 0)] + [(step, NT - 1) for step in (down_y, finish)]
                for step, n in steps:
                    step(n)

            def group(g, more):
                for u in range(QN, NU):
                    gate_up(g, u, more)
                down(g, more)
                if more:
                    for u in range(QN):
                        gate_up(g + 1, u, True)

            gate_up(0, 0, True)
            thresholds(2)
            link(nc.vector.tensor_scalar(osc[:, :], thr[:, 0:1], thr[:, 1:2], 8.0 / HS, ALU.mult, ALU.mult))
            link(nc.vector.tensor_tensor(osc[:, :], osc[:, :], thr[:, 2:3], ALU.mult))
            ternary(2)
            gate_up(0, 1, True, lambda: halves(0))
            weight_slots(0, P, HW, slots_ready)
            half, rest = slice(0, NS // 2), slice(NS // 2, NS)
            gate_up(0, 2, True, lambda: weight_slots(1, P, HW, None, half))
            weight_slots(1, P, HW, slots_ready, rest)
            gate_up(0, 3, True, lambda: weight_slots(2, 0, NC * DB, None, half))
            weight_slots(2, 0, NC * DB, down_ready, rest)
            with dve.Fori(0, G - 1) as g:
                group(g, True)
            group(G - 1, False)

            dve.wait_ge(flag_done, 1)
            rows_left = dve.value_load(flag[0:1, 0:1])
            with dve.If(rows_left > 0):
                with dve.Fori(0, ROWS // P) as n:
                    step = [0]

                    def then(ins):
                        step[0] += 1
                        ins.then_inc(s_sem["dve"], 1)
                        dve.wait_ge(s_sem["dve"], STEPS * n + step[0])
                        dve.sem_inc(dve_tick, 1)

                    col = lambda i: slow_st[:, i:i + 1]
                    xx = slow_xx[:, 0:D]
                    dve.wait_ge(s_sem["x_in"], 32 * n + 32)
                    then(nc.vector.tensor_reduce(col(0), slow_x, AX.X, ALU.add))
                    then(nc.vector.tensor_scalar_mul(col(1), col(0), 1.0 / D))
                    then(nc.vector.tensor_scalar(slow_acc, slow_x, col(1), None, ALU.subtract))
                    then(nc.vector.scalar_tensor_tensor(slow_junk, slow_acc, 1.0, slow_acc, ALU.mult, ALU.mult, accum_out=col(2)))
                    then(nc.vector.tensor_scalar(col(3), col(2), 1.0 / D, EPS, ALU.mult, ALU.add))
                    then(nc.vector.tensor_scalar(col(5).bitcast(I32), col(3).bitcast(I32), 1, None, ALU.arith_shift_right))
                    then(nc.vector.tensor_copy(col(6), col(5).bitcast(I32)))
                    then(nc.vector.tensor_scalar(col(6), col(6), -1.0, float(0x5F3759DF), ALU.mult, ALU.add))
                    then(nc.vector.tensor_copy(col(5).bitcast(I32), col(6)))
                    for _ in range(4):
                        then(nc.vector.tensor_tensor(col(6), col(5), col(5), ALU.mult))
                        then(nc.vector.tensor_tensor(col(6), col(6), col(3), ALU.mult))
                        then(nc.vector.tensor_scalar(col(6), col(6), -0.5, 1.5, ALU.mult, ALU.add))
                        then(nc.vector.tensor_tensor(col(5), col(5), col(6), ALU.mult))
                    then(nc.vector.tensor_scalar(xx, slow_acc, col(5), None, ALU.mult))
                    then(nc.vector.tensor_copy(slow_xx[:, D:2 * D], xx))
                    with dve.Fori(0, D) as d:
                        nc.vector.tensor_tensor(slow_junk, xx, slow_xx[:, bass.ds(d, D)], ALU.mult).then_inc(s_lag, 1)
                        dve.wait_ge(s_lag, D * 2 * n + 2 * d + 1)
                        nc.vector.tensor_reduce(slow_corr[:, bass.ds(d, 1)], slow_junk, AX.X, ALU.add).then_inc(s_lag, 1)
                        dve.wait_ge(s_lag, D * 2 * n + 2 * d + 2)
                        dve.nop()
                    then(nc.vector.max(slow_top, slow_corr))
                    then(nc.vector.tensor_scalar_mul(slow_neg, slow_top[:, 0:1], -1.0))
                    then(nc.vector.memset(slow_top[:, TOP:8], 3.0e38))
                    then(nc.vector.match_replace(slow_mask, slow_top, slow_corr, -3.0e38))
                    nc.vector.tensor_scalar(slow_mask, slow_mask, -3.0e38, None, ALU.is_equal).then_inc(s_sem["ex_in"], 1)
                    dve.wait_ge(s_sem["act"], n + 1)
                    dve.wait_ge(s_sem["ex_in"], n + 1)
                    then(nc.vector.scalar_tensor_tensor(slow_w, slow_w, 1.0, slow_mask, ALU.mult, ALU.mult, accum_out=col(7)))
                    then(nc.vector.reciprocal(col(8), col(7)))
                    then(nc.vector.tensor_scalar(slow_w, slow_w, col(8), None, ALU.mult))
                    then(nc.vector.tensor_scalar(slow_acc, xx, -1.0, None, ALU.mult))
                    with dve.Fori(0, D) as d:
                        nc.vector.tensor_scalar(slow_junk, slow_xx[:, bass.ds(d, D)], slow_w[:, bass.ds(d, 1)], None, ALU.mult).then_inc(s_add, 1)
                        dve.wait_ge(s_add, D * 2 * n + 2 * d + 1)
                        nc.vector.tensor_tensor(slow_acc, slow_acc, slow_junk, ALU.add).then_inc(s_add, 1)
                        dve.wait_ge(s_add, D * 2 * n + 2 * d + 2)
                        dve.nop()
                    nc.vector.tensor_tensor(slow_out, slow_out, slow_acc, ALU.add).then_inc(s_sem["ob"], 1)
                    dve.nop()
            dve.nop()

        @block.gpsimd
        def _(pool):
            nc.gpsimd.memset(ident[:, :], 0.0).then_inc(pchain, 1)
            nc.gpsimd.memset(ident16[:, :], 0.0).then_inc(pchain, 1)
            nc.gpsimd.memset(ones[:, :], 1.0).then_inc(const_done, 1)
            pool.wait_ge(pchain, 2)
            for m in (ident, ident16):
                nc.gpsimd.affine_select(out=m[:, :], in_=m[:, :], compare_op=ALU.not_equal, fill=1.0, base=0,
                                        pattern=[[-1, P]], channel_multiplier=1).then_inc(const_done, 1)

            def guess(n):
                pool.wait_ge(v_done, 5 * n + 1)
                nc.gpsimd.tensor_tensor(r0[:, :], vr[:, :], mh[:, :], ALU.pow).then_inc(guess_done, 1)

            def normalise(n, first=0):
                pool.wait_ge(v_done, 5 * n + 5)
                pool.sem_inc(pool_tick, 1)
                for t in range(first, NT):
                    nc.gpsimd.tensor_scalar(xr[:, t, :], xr[:, t, :], nm[:, t:t + 1], rs[:, t:t + 1], ALU.add, ALU.mult).then_inc(ln_done, 1)

            def split_pair(base, q):
                pool.wait_ge(tr_sumhi, base + q + 1)
                nc.gpsimd.tensor_tensor(xop[:, q, 2, 1, :], ss[:, q % 2, :], xop[:, q, 2, 0, :], ALU.subtract).then_inc(x_ready, 1)

            for m in range(2):
                pool.wait_ge(thr_done, m + 1)
                pool.sem_inc(pool_tick, 1)
                src, _, neg = parts[m][1]
                nc.gpsimd.tensor_scalar(neg, src, nthr[0:last_rows, m:m + 1], None, ALU.is_lt).then_inc(neg_done, 1)

            guess(0)
            normalise(0, NT // 2)
            for q in range(QN):
                split_pair(0, q)
            nc.gpsimd.memset(pz[:, :], 0.0).then_inc(h_ready, 1)

            def gate_up(g, u):
                c, k = divmod(u, QN)
                pool.wait_ge(h_done, NU * g + u + 1)
                nc.gpsimd.tensor_tensor(hh[:, 2, :], hh[:, 0, :], hh[:, 1, :], ALU.add).then_inc(h_sum, 1)
                pool.wait_ge(h_hi, NU * g + u + 1)
                nc.gpsimd.tensor_tensor(hop[0:CH, c, k, :, 1, :], hh[:, :, :], hop[0:CH, c, k, :, 0, :], ALU.subtract).then_inc(h_ready, 1)

            def down(g, more):
                def residual(t):
                    if t:
                        pool.wait_ge(z_done, NT * g + t)
                    pool.wait_ge(zx_in[t % 2], 16 * (NT // 2 * g + t // 2 + 1))
                    pool.sem_inc(pool_tick, 1)
                    nc.gpsimd.tensor_scalar(zt[:, :], zx[:, t % 2, :], nmd[:, t:t + 1], rsd[:, t:t + 1], ALU.add, ALU.mult).then_inc(z_part, 1)
                    pool.wait_ge(z_part, NT * g + t + 1)
                    nc.gpsimd.tensor_tensor(zx[:, t % 2, :], zx[:, t % 2, :], zt[:, :], ALU.add).then_inc(z_done, 1)

                def split(q):
                    split_pair(QN * g + QN, q)

                if more:
                    steps = [(residual, 0), (residual, 1), (split, 0), (split, 1), (residual, 2), (split, 2), (residual, 3), (split, 3)]
                else:
                    steps = [(residual, t) for t in range(NT)]
                for step, n in steps:
                    step(n)

            def group(g, more):
                for u in range(QN, NU):
                    gate_up(g, u)
                if more:
                    guess(g + 1)
                    normalise(g + 1)
                down(g, more)
                if more:
                    for u in range(QN):
                        gate_up(g + 1, u)

            for u in range(QN):
                gate_up(0, u)
            with pool.Fori(0, G - 1) as g:
                group(g, True)
            group(G - 1, False)


def kernel(L0_attn_x, L0_ffn_w_gate, L0_ffn_w_up, L0_ffn_w_down):
    import numpy as _np
    import concourse.bacc as _bacc
    from concourse import mybir as _mybir
    from concourse.bass_utils import run_bass_kernel_spmd as _run

    L, P = 1024, 128
    f = _np.arange(1, L // 4, 2)[None, :]
    t = _np.arange(L // 4)[:, None]
    angle = 2.0 * _np.pi * ((t * f) % 512) / 512.0
    dft = _np.concatenate([_np.cos(angle), _np.sin(angle)], axis=1).astype(_np.float16)
    dft = _np.ascontiguousarray(dft.reshape(2, P, 256).transpose(1, 0, 2))
    d = _np.arange(1, 257)[None, :]
    lag = 2.0 * (1.0 - _np.cos(2.0 * _np.pi * ((f.reshape(P, 1) * d) % 512) / 512.0))
    lag = _np.concatenate([lag, lag], axis=0).astype(_np.float16)
    lag = _np.ascontiguousarray(lag.reshape(2, P, 256).transpose(1, 0, 2))

    arrays = {
        "in_x": _np.ascontiguousarray(_np.asarray(L0_attn_x)[0]),
        "in_w_gate": _np.ascontiguousarray(L0_ffn_w_gate),
        "in_w_up": _np.ascontiguousarray(L0_ffn_w_up),
        "in_w_down": _np.ascontiguousarray(L0_ffn_w_down),
        "in_dft": dft,
        "in_lag": lag,
    }
    nc = _bacc.Bacc("TRN2", target_bir_lowering=False, num_devices=1)
    args = [nc.dram_tensor(n, a.shape, _mybir.dt.from_np(a.dtype), kind="ExternalInput").ap() for n, a in arrays.items()]
    out = nc.dram_tensor("out_y", (2048, L), _mybir.dt.float32, kind="ExternalOutput").ap()
    octonion_ffn_attention_kernel(nc, *args, out)
    r = _run(nc, [arrays], core_ids=[0])
    return r.results[0]["out_y"].reshape(1, 2048, L)
```
